# Optimizing a Trainium2 kernel written in Bass

```python
import numpy as np
import jax
import jax.numpy as jnp

def _softmax(x, axis=-1):
    return jax.nn.softmax(x, axis=axis)

def _gelu(x):
    return jax.nn.gelu(x, approximate=True)

def _silu(x):
    return jax.nn.silu(x)

def _sigmoid(x):
    return jax.nn.sigmoid(x)

def _layernorm(x, axis=-1, eps=1e-05):
    m = jnp.mean(x, axis=axis, keepdims=True)
    v = jnp.var(x, axis=axis, keepdims=True)
    return (x - m) / jnp.sqrt(v + eps)

def _scatter_add(tgt, idx, src, axis=0):
    return tgt.at[idx].add(src)

def _segment_sum(src, seg, n):
    return jax.ops.segment_sum(src, seg, n)
kernel_name = 'mk_gnn_preln_d1_gnn_r8_6d69e6'

def setup_inputs(seed: int=0):
    np.random.seed(seed)
    _w = jnp.asarray

    def _rec_inputs():
        import jax
        import jax.numpy as jnp
        _gk = jax.random.key(seed)
        x = -0.0005121 + 1.001 * jax.random.normal(jax.random.fold_in(_gk, 1), (6250, 64), jnp.float32)
        src = jax.random.randint(jax.random.fold_in(_gk, 2), (200000,), 0, 6250, jnp.int32)
        dst = jnp.minimum((6250 * jax.random.uniform(jax.random.fold_in(_gk, 3), (200000,)) ** 2.0).astype(jnp.int32), 49999)
        _o = jnp.argsort(dst, stable=True)
        src = src[_o]
        dst = dst[_o]
        edge_attr_8 = -4.12889e-05 + 1 * jax.random.normal(jax.random.fold_in(_gk, 12), (200000, 8), jnp.float32)
        return (x, src, dst, edge_attr_8)
    x, src, dst, edge_attr_8 = _rec_inputs()

    def _L0_gnn_setup():
        import jax, jax.numpy as jnp
        import numpy as np
        N_NODES = 6250
        N_EDGES = 100000
        D = 64
        N_BASIS = 8
        key = jax.random.key(seed)
        ks = jax.random.split(key, 16)
        inp = {'p': jax.random.normal(ks[0], (N_NODES, D), dtype=jnp.float32), 'idx_i': jax.random.randint(ks[1], (N_EDGES,), 0, N_NODES), 'idx_j': jax.random.randint(ks[2], (N_EDGES,), 0, N_NODES), 'basis': jax.random.normal(ks[3], (N_EDGES, N_BASIS), dtype=jnp.float32), 'pp_W1': jax.random.normal(ks[4], (D, D), dtype=jnp.float32) / np.sqrt(D), 'pp_b1': jnp.zeros((D,), dtype=jnp.float32), 'pp_W2': jax.random.normal(ks[5], (D, D), dtype=jnp.float32) / np.sqrt(D), 'pp_b2': jnp.zeros((D,), dtype=jnp.float32), 'pi_W1': jax.random.normal(ks[6], (2 * D, D), dtype=jnp.float32) / np.sqrt(2 * D), 'pi_b1': jnp.zeros((D,), dtype=jnp.float32), 'pi_W2': jax.random.normal(ks[7], (D, D), dtype=jnp.float32) / np.sqrt(D), 'pi_b2': jnp.zeros((D,), dtype=jnp.float32), 'pi_W3': jax.random.normal(ks[8], (D, D * N_BASIS), dtype=jnp.float32) / np.sqrt(D), 'ii_W1': jax.random.normal(ks[9], (D, D), dtype=jnp.float32) / np.sqrt(D), 'ii_b1': jnp.zeros((D,), dtype=jnp.float32), 'ii_W2': jax.random.normal(ks[10], (D, D), dtype=jnp.float32) / np.sqrt(D), 'ii_b2': jnp.zeros((D,), dtype=jnp.float32)}
        return inp
    _L0_gnn_all = _L0_gnn_setup()
    _L0_gnn_in = {k: v for k, v in _L0_gnn_all.items() if k in ('pp_W1', 'pp_b1', 'pp_W2', 'pp_b2', 'pi_W1', 'pi_b1', 'pi_W2', 'pi_b2', 'pi_W3', 'ii_W1', 'ii_b1', 'ii_W2', 'ii_b2')}
    del _L0_gnn_all
    return {'x': x, 'src': src, 'dst': dst, 'edge_attr_8': edge_attr_8, 'L0_gnn_pp_W1': _L0_gnn_in['pp_W1'], 'L0_gnn_pp_b1': _L0_gnn_in['pp_b1'], 'L0_gnn_pp_W2': _L0_gnn_in['pp_W2'], 'L0_gnn_pp_b2': _L0_gnn_in['pp_b2'], 'L0_gnn_pi_W1': _L0_gnn_in['pi_W1'], 'L0_gnn_pi_b1': _L0_gnn_in['pi_b1'], 'L0_gnn_pi_W2': _L0_gnn_in['pi_W2'], 'L0_gnn_pi_b2': _L0_gnn_in['pi_b2'], 'L0_gnn_pi_W3': _L0_gnn_in['pi_W3'], 'L0_gnn_ii_W1': _L0_gnn_in['ii_W1'], 'L0_gnn_ii_b1': _L0_gnn_in['ii_b1'], 'L0_gnn_ii_W2': _L0_gnn_in['ii_W2'], 'L0_gnn_ii_b2': _L0_gnn_in['ii_b2']}

def reference(x, src, dst, edge_attr_8, L0_gnn_pp_W1, L0_gnn_pp_b1, L0_gnn_pp_W2, L0_gnn_pp_b2, L0_gnn_pi_W1, L0_gnn_pi_b1, L0_gnn_pi_W2, L0_gnn_pi_b2, L0_gnn_pi_W3, L0_gnn_ii_W1, L0_gnn_ii_b1, L0_gnn_ii_W2, L0_gnn_ii_b2):
    import jax
    import jax.numpy as jnp

    def _L0_gnn_ref(p, idx_i, idx_j, basis, pp_W1, pp_b1, pp_W2, pp_b2, pi_W1, pi_b1, pi_W2, pi_b2, pi_W3, ii_W1, ii_b1, ii_W2, ii_b2):
        import jax, jax.numpy as jnp
        import numpy as np
        N_NODES = 6250
        N_EDGES = 100000
        D = 64
        N_BASIS = 8
        p1 = jnp.tanh(p @ pp_W1 + pp_b1) @ pp_W2 + pp_b2
        inter = jnp.concatenate([p1[idx_i], p1[idx_j]], axis=-1)
        inter = inter @ pi_W1 + pi_b1
        inter = inter @ pi_W2 + pi_b2
        inter = inter @ pi_W3
        inter = inter.reshape(inter.shape[0], D, N_BASIS)
        i1 = jnp.einsum('ecb,eb->ec', inter, basis)
        i1 = jnp.tanh(i1 @ ii_W1 + ii_b1) @ ii_W2 + ii_b2
        out = jax.ops.segment_sum(i1, idx_j, num_segments=p1.shape[0])
        return out
    h = jnp.maximum(_layernorm(x, axis=-1), 0.0)
    x = x + _L0_gnn_ref(h, src, dst, edge_attr_8, L0_gnn_pp_W1, L0_gnn_pp_b1, L0_gnn_pp_W2, L0_gnn_pp_b2, L0_gnn_pi_W1, L0_gnn_pi_b1, L0_gnn_pi_W2, L0_gnn_pi_b2, L0_gnn_pi_W3, L0_gnn_ii_W1, L0_gnn_ii_b1, L0_gnn_ii_W2, L0_gnn_ii_b2)
    return x

_drawn_inputs = setup_inputs


def setup_inputs(seed=0):
    import zlib

    import numpy as np

    out = dict(_drawn_inputs(seed))
    spreads = {'L0_gnn_pp_b1': (0.0, 0.1),
     'L0_gnn_pp_b2': (0.0, 0.1),
     'L0_gnn_pi_b1': (0.0, 0.1),
     'L0_gnn_pi_b2': (0.0, 0.1),
     'L0_gnn_ii_b1': (0.0, 0.1),
     'L0_gnn_ii_b2': (0.0, 0.1)}
    factors = {}
    for name, (base, spread) in spreads.items():
        noise = np.random.default_rng([zlib.crc32(name.encode()), seed]).standard_normal(out[name].shape)
        drawn = base * np.exp(spread * noise) if base else spread * noise
        out[name] = jnp.asarray(drawn.astype(out[name].dtype))
    for name, factor in factors.items():
        out[name] = (out[name] * factor).astype(out[name].dtype)
    return out
```

```python
from contextlib import ExitStack

import numpy as np

import concourse.bass as bass
from concourse import mybir


def program(nc, x, src, dst, edge_attr, pp_W1, pp_b1, pp_W2, pp_b2, pi_W1, pi_b1, pi_W2, pi_b2, pi_W3,
            ii_W1, ii_b1, ii_W2, ii_b2, out, u_tab, v_tab, loc_tab):
    f32, i32, u32, bf16 = mybir.dt.float32, mybir.dt.int32, mybir.dt.uint32, mybir.dt.bfloat16
    ALU, ACT, AX = mybir.AluOpType, mybir.ActivationFunctionType, mybir.AxisListType

    N, D = x.shape
    E, NB = edge_attr.shape
    P = 128
    EPS = 1e-5

    NPP = 50
    NP = N // NPP
    CH = 4
    CHUNKS = [(c, min(CH, NPP - c)) for c in range(0, NPP, CH)]

    TILES = 4
    GE = P * TILES
    UN = 4
    NG = -(-E // (GE * UN)) * UN
    ITERS = NG // UN
    FULL = E // GE
    PART = (E - FULL * GE) // TILES
    RB = 4
    RQ = NG // RB
    W = 64
    BW = 512
    NBLK = -(-N // BW)
    F = NB * D
    FC = F // P
    SPLIT_IT = ITERS // 2 - 1
    SPLIT = UN * (SPLIT_IT + 1)
    EARLY = 4 * UN

    assert NP * NPP == N and RQ * RB == NG and RQ <= P and PART * TILES + FULL * GE == E and F == FC * P

    ctx = ExitStack()
    with ctx:
        def sb(name, shape, dt=f32):
            return ctx.enter_context(nc.sbuf_tensor(name, shape, dt))

        def sem(name):
            return ctx.enter_context(nc.semaphore(name))

        def sems(name, n):
            return [sem(f"{name}{i}") for i in range(n)]

        x_sb = sb("x_sb", [NP, NPP * D])
        basis = sb("basis", [P, NG * TILES * NB])
        src_e = sb("src_e", [P, (NG + UN) * TILES], i32)
        dst_e = sb("dst_e", [P, NG * TILES])
        loc_e = sb("loc_e", [P, NG * TILES])
        base_row = sb("base_row", [1, NG], i32)
        acc_full = sb("acc_full", [P, NBLK * BW])
        acc = acc_full[0:D + 1, :]
        ident = sb("ident", [P, P])
        iota_f = sb("iota_f", [P, BW])
        iota_p = sb("iota_p", [P, 1])
        g_sb = sb("g_sb", [P, FC, D])
        w_out = sb("w_out", [D + 1, D])
        bias_l = sb("bias_l", [96, P], bf16)
        bias_r = sb("bias_r", [96, TILES * D], bf16)
        fast = sb("fast", [1, 1], i32)

        idx_u = sb("idx_u", [P, UN, TILES], i32)
        idx_v = sb("idx_v", [P, TILES], i32)
        u_rows = sb("u_rows", [P, UN, TILES, D])
        v_rows = sb("v_rows", [P, TILES, D])
        v_win = sb("v_win", [W, UN, D])
        loc_bc = sb("loc_bc", [P, UN, GE])
        hot_t = sb("hot_t", [W, 2, GE])
        hot = sb("hot", [P, UN, TILES, W])
        s_sb = sb("s_sb", [P, 2, TILES, D])
        o_sb = sb("o_sb", [P, 2, TILES, NB, D])
        ot_sb = sb("ot_sb", [P, TILES, F])
        t_sb = sb("t_sb", [P, 2, TILES, D + 1])
        dcur = sb("dcur", [P, TILES])

        w1 = sb("w1", [D, D])
        p2 = sb("p2", [D, D])
        iw1 = sb("iw1", [D, D])
        wraw = sb("wraw", [D, 3, D])
        w3 = sb("w3", [D, D * NB])
        wt = sb("wt", [D, 2, D])
        w2t = sb("w2t", [D, D + 1])
        a12 = sb("a12", [D, 2, D])
        w3t = sb("w3t", [D, F])
        c1 = sb("c1", [D, D + 1])
        c2 = sb("c2", [1, D + 1])
        b2row = sb("b2row", [1, D])
        b1col = sb("b1col", [D, 1])
        uvw = sb("uvw", [D + 1, 2 * D])
        brow = sb("brow", [96, 2, D])
        bpart = sb("bpart", [96, D], bf16)
        stats = sb("stats", [NP, 4, NPP])
        h_t = sb("h_t", [D, 2, CH * NP])
        a_t = sb("a_t", [D + 1, 2, CH * NP])
        uv_sb = sb("uv_sb", [NP, 2, 2, CH, D])
        rowst = sb("rowst", [RQ, 4, RB])
        span1 = sb("span1", [1, 2])
        base_f = sb("base_f", [1, NG])
        ones1 = sb("ones1", [1, P])
        loc_rows = sb("loc_rows", [RQ, RB, TILES, P])
        xc = o_sb[0:NP, :, :, :, :].rearrange("p a t b k -> p (a t b k)")[:, 0:NPP * D]
        src_raw = ot_sb[0:RQ, :, :].bitcast(i32)
        src_rows = ot_sb[0:RQ, :, :]
        dst_raw = loc_bc[0:RQ, :, :].bitcast(i32)
        dst_rows = loc_bc[0:RQ, :, :]
        xsq = acc_full[0:NP, 0:NPP * D]
        hot_blk = o_sb[:, 0, :, :, :].rearrange("p t b k -> p t (b k)")

        bank = [ctx.enter_context(nc.psum_tensor(f"bank{i}", [P, 512], f32)) for i in range(8)]
        ot_ps = bank[0:4]
        sv_ps = [bank[i][:, 0:TILES * D].rearrange("p (t k) -> p t k", t=TILES) for i in (4, 5)]
        z_ps = bank[6]
        seg_ps = bank[7][0:D + 1, 0:W]

        x_in = sem("x_in")
        weights_in = sem("weights_in")
        padded = sem("padded")
        consts = sem("consts")
        rows_in = sem("rows_in")
        basis_in = sems("basis_in", 3)
        ln = sem("ln")
        sq_done = sem("sq_done")
        prep = sem("prep")
        wprep_pe = sem("wprep_pe")
        wprep_dve = sem("wprep_dve")
        ht_ps_ready = sem("ht_ps_ready")
        ht_ready = sem("ht_ready")
        a_ps_ready = sem("a_ps_ready")
        a_ready = sem("a_ready")
        uv_ps_ready = sem("uv_ps_ready")
        uv_ready = sem("uv_ready")
        tables_out = [sem(f"tables_out{i}") for i in range(2)]
        loc_out = sem("loc_out")
        cols_ps = sem("cols_ps")
        cols_read = sem("cols_read")
        flag_ready = sem("flag_ready")
        zeroed = sem("zeroed")
        held = sem("held")

        idx_ready = sems("idx_ready", UN)
        u_in = sems("u_in", UN)
        v_in = sems("v_in", UN)
        loc_in = sems("loc_in", UN)
        hot_t_ready = sems("hot_t_ready", UN)
        hot_ready = sems("hot_ready", UN)
        sv_ready = sems("sv_ready", UN)
        s_ready = sems("s_ready", UN)
        o_ready = sems("o_ready", UN)
        ot_ready = [sems(f"ot_ready{k}_", TILES) for k in range(UN)]
        ot_copied = [sems(f"ot_copied{k}_", TILES) for k in range(UN)]
        z_ready = sems("z_ready", UN)
        t_ready = sems("t_ready", UN)
        seg_ready = sems("seg_ready", UN)
        acc_done = sems("acc_done", UN)

        g_idx = sem("g_idx")
        g_rows = sem("g_rows")
        g_o = sem("g_o")
        g_ot = sem("g_ot")
        g_otc = sem("g_otc")
        g_z = sem("g_z")
        g_t = sem("g_t")
        g_hot = sem("g_hot")
        g_seg = sem("g_seg")
        g_dve = sem("g_dve")

        acc_ready = sem("acc_ready")
        y_ps = sem("y_ps")
        y_ready = sem("y_ready")
        stored = sem("stored")

        block = ctx.enter_context(nc.Block())

        def slot(u, lag):
            return (u - lag) % UN

        def count(it, u, lag):
            return it + 2 + (u - lag) // UN

        def dma_count(it, u, lag):
            return it + 1 + (u - lag) // UN

        def has(u, lag, first, last):
            return (not first or u >= lag) and (not last or u < lag)

        def windowed(eng, body, halves=False):
            body(0, True, False)
            if halves:
                with eng.Fori(1, SPLIT_IT) as it:
                    body(it, False, False)
                eng.wait_ge(basis_in[2], 32)
                with eng.Fori(SPLIT_IT, ITERS) as it:
                    body(it, False, False)
            else:
                with eng.Fori(1, ITERS) as it:
                    body(it, False, False)
            body(ITERS, False, True)

        N_TAB = [16 * len(CHUNKS[i::2]) * 2 for i in range(2)]
        N_WEIGHT_DMAS = 16

        @block.sync
        def _(sp):
            xv = x.rearrange("(p i) d -> p (i d)", i=NPP)
            sp.dma_start(x_sb[:, :], xv).then_inc(x_in, 16)
            sp.wait_ge(padded, 1)
            for raw, idx in ((src_raw, src), (dst_raw, dst)):
                whole = (RB - 1) * RQ
                sp.dma_start(raw[:, 0:RB - 1, :], idx[0:whole * GE].rearrange(
                    "(b q e) -> q b e", b=RB - 1, e=GE)).then_inc(rows_in, 16)
                sp.dma_start(raw[0:FULL - whole, RB - 1, :], idx[whole * GE:FULL * GE].rearrange(
                    "(q e) -> q e", e=GE)).then_inc(rows_in, 16)
                sp.dma_start(raw[FULL - whole:FULL - whole + 1, RB - 1, 0:E - FULL * GE],
                             idx[FULL * GE:E].rearrange("(q e) -> q e", q=1)).then_inc(rows_in, 16)
            bv = basis[:, :].rearrange("p (g f) -> p g f", g=NG)
            for (lo, hi), done in zip(((0, EARLY), (EARLY, SPLIT), (SPLIT, FULL)), basis_in):
                sp.dma_start(bv[:, lo:hi, :], edge_attr[lo * GE:hi * GE, :].rearrange(
                    "(g p j) b -> p g (j b)", p=P, j=TILES)).then_inc(done, 16)
            sp.dma_start(bv[0:PART, FULL, :], edge_attr[FULL * GE:E, :].rearrange(
                "(p j) b -> p (j b)", j=TILES)).then_inc(basis_in[2], 16)
            sp.wait_ge(prep, 11)
            sp.dma_start(loc_tab.rearrange("(b q) e -> q b e", b=RB),
                         loc_rows[:, :, :, :].rearrange("q b j p -> q b (j p)")).then_inc(loc_out, 16)
            u_v = u_tab.rearrange("(p i) d -> p i d", i=NPP)
            v_v = v_tab.rearrange("(p i) d -> p i d", i=NPP)
            for c, (i0, n) in enumerate(CHUNKS):
                sp.wait_ge(uv_ready, c + 1)
                sp.dma_start(u_v[:, i0:i0 + n, :], uv_sb[:, c % 2, 0, 0:n, :]).then_inc(tables_out[c % 2], 16)
                sp.dma_start(v_v[:, i0:i0 + n, :], uv_sb[:, c % 2, 1, 0:n, :]).then_inc(tables_out[c % 2], 16)

            sp.wait_ge(tables_out[0], N_TAB[0])
            sp.wait_ge(tables_out[1], N_TAB[1])
            sp.wait_ge(loc_out, 16)
            sp.wait_ge(cols_read, 2 * TILES + 3)
            sp.wait_ge(flag_ready, 1)
            is_fast = sp.value_load(fast[0:1, 0:1], min_val=0, max_val=1)

            def body(it, first, last):
                for u in range(UN):
                    if has(u, 0, first, last):
                        start = sp.value_load(base_row[0:1, bass.ds(it * UN + u, 1)], min_val=0, max_val=N - W)
                        if not first:
                            sp.wait_ge(hot_t_ready[u], count(it, u, UN))
                        sp.dma_start(loc_bc[0:W, u, :], loc_tab[bass.ds(it * UN + u, 1), :].to_broadcast(
                            [W, GE])).then_inc(loc_in[u], 16)
                        if not first:
                            sp.wait_ge(sv_ready[u], count(it, u, UN))
                        sp.dma_start(v_win[:, u, :], v_tab[bass.ds(start, W), :]).then_inc(v_in[u], 16)

            with sp.If(is_fast):
                windowed(sp, body)

            ov = out.rearrange("(p i) d -> p (i d)", i=NPP)
            half = 24 * D
            sp.wait_ge(y_ready, 3)
            sp.dma_start(ov[:, 0:half], x_sb[:, 0:half]).then_inc(stored, 16)
            sp.wait_ge(y_ready, 7)
            sp.dma_start(ov[:, half:], x_sb[:, half:]).then_inc(stored, 16)
            sp.wait_ge(stored, 32)

        @block.gpsimd
        def _(pool):
            nc.gpsimd.memset(src_raw[:, RB - 1, :], 0)
            nc.gpsimd.memset(dst_raw[:, RB - 1, :], N)
            nc.gpsimd.memset(basis[:, FULL * TILES * NB:], 0.0)
            pool.drain().then_inc(padded, 1)
            nc.gpsimd.memset(ident[:], 0.0).then_inc(zeroed, 1)
            pool.wait_ge(zeroed, 1)
            nc.gpsimd.affine_select(out=ident[:], in_=ident[:], compare_op=ALU.not_equal, fill=1.0, base=0,
                                    pattern=[[-1, P]], channel_multiplier=1).then_inc(consts, 1)
            nc.gpsimd.memset(c1[:], 0.0)
            nc.gpsimd.memset(c2[:], 0.0)
            nc.gpsimd.memset(ones1[:], 1.0)
            nc.gpsimd.memset(a_t[:], 1.0)
            nc.gpsimd.memset(brow[:], 0.0)
            pool.drain().then_inc(consts, 1)
            nc.gpsimd.memset(c2[:, D:D + 1], 1.0)
            nc.gpsimd.iota(iota_f[:], pattern=[[1, BW]], base=0, channel_multiplier=0,
                           allow_small_or_imprecise_dtypes=True)
            nc.gpsimd.iota(iota_p[:], pattern=[[0, 1]], base=0, channel_multiplier=1,
                           allow_small_or_imprecise_dtypes=True)
            nc.gpsimd.memset(bias_l[:], 1.0)
            nc.gpsimd.memset(t_sb[:], 1.0)
            pool.wait_ge(ln, 4)
            nc.gpsimd.memset(acc, 0.0)
            nc.gpsimd.memset(src_e[:, NG * TILES:], 0)
            pool.drain().then_inc(consts, 1)

            pool.wait_ge(tables_out[0], N_TAB[0])
            pool.wait_ge(tables_out[1], N_TAB[1])
            pool.wait_ge(flag_ready, 1)
            is_fast = pool.value_load(fast[0:1, 0:1], min_val=0, max_val=1)

            def body(it, first, last):
                for u in range(UN):
                    if has(u, 0, first, last):
                        pool.wait_ge(idx_ready[u], dma_count(it, u, 0))
                        if not first:
                            pool.wait_ge(s_ready[u], count(it, u, UN))
                        pool.sem_inc(held, 1)
                        for j in range(TILES):
                            pool.indirect_dma_start(
                                out=u_rows[:, u, j, :], out_offset=None, in_=u_tab[:, :],
                                in_offset=bass.IndirectOffsetOnAxis(ap=idx_u[:, u, j:j + 1].bitcast(u32), axis=0),
                            ).then_inc(u_in[u], 16)

            with pool.If(is_fast):
                windowed(pool, body)
            with pool.Else():
                with pool.Fori(0, NG) as g:
                    pool.wait_ge(g_idx, g + 1)
                    pool.sem_inc(held, 1)
                    for j in range(TILES):
                        for rows, tab, idx in ((u_rows[:, 0], u_tab, idx_u[:, 0]), (v_rows, v_tab, idx_v)):
                            pool.indirect_dma_start(
                                out=rows[:, j, :], out_offset=None, in_=tab[:, :],
                                in_offset=bass.IndirectOffsetOnAxis(ap=idx[:, j:j + 1].bitcast(u32), axis=0),
                            ).then_inc(g_rows, 16)

        @block.scalar
        def _(act):
            loads = [(wraw[:, 0, :], pp_W2), (wraw[:, 1, :], pi_W1[0:D, :]), (wraw[:, 2, :], pi_W1[D:2 * D, :]),
                     (p2[:], pi_W2), (w1[:], pp_W1), (b1col[:], pp_b1.rearrange("(p a) -> p a", a=1)),
                     (w2t[:, D:D + 1], pp_b2.rearrange("(p a) -> p a", a=1)),
                     (b2row[:], pi_b2.rearrange("(a d) -> a d", a=1)),
                     (w3[:], pi_W3), (iw1[:], ii_W1), (w_out[0:D, :], ii_W2),
                     (w_out[D:D + 1, :], ii_b2.rearrange("(a d) -> a d", a=1))]
            for dest, source in loads:
                act.dma_start(dest, source).then_inc(weights_in, 16)
            act.wait_ge(consts, 2)
            act.dma_start(c1[:, D:D + 1], pi_b1.rearrange("(p a) -> p a", a=1)).then_inc(weights_in, 16)
            for r in range(3):
                act.dma_start(brow[32 * r:32 * r + 1, 0, :], ii_b1.rearrange("(a d) -> a d", a=1)).then_inc(
                    weights_in, 16)

            act.wait_ge(ln, 5)
            nc.scalar.activation(stats[:, 2, :], stats[:, 1, :], ACT.Sqrt).then_inc(sq_done, 1)

            for c in range(len(CHUNKS) + 2):
                if c < len(CHUNKS):
                    i0, n = CHUNKS[c]
                    act.wait_ge(ht_ps_ready, c + 1)
                    if c >= 2:
                        act.wait_ge(a_ps_ready, c - 1)
                    nc.scalar.activation(h_t[:, c % 2, 0:n * NP], bank[c % 2][0:D, 0:n * NP],
                                         ACT.Relu).then_inc(ht_ready, 1)
                if 1 <= c <= len(CHUNKS):
                    k = c - 1
                    i0, n = CHUNKS[k]
                    act.wait_ge(a_ps_ready, k + 1)
                    act.wait_ge(weights_in, 16 * N_WEIGHT_DMAS)
                    if k >= 2:
                        act.wait_ge(uv_ps_ready, k - 1)
                    nc.scalar.activation(a_t[0:D, k % 2, 0:n * NP], bank[2 + k % 2][0:D, 0:n * NP], ACT.Tanh,
                                         bias=b1col[:, 0:1]).then_inc(a_ready, 1)
                if c >= 2:
                    k = c - 2
                    i0, n = CHUNKS[k]
                    act.wait_ge(uv_ps_ready, k + 1)
                    if k >= 2:
                        act.wait_ge(tables_out[k % 2], 32 * (k // 2))
                    nc.scalar.activation(
                        uv_sb[:, k % 2, :, 0:n, :].rearrange("p w i d -> p i w d"),
                        bank[4 + k % 2][0:NP, 0:n * 2 * D].rearrange("p (i w d) -> p i w d", w=2, d=D),
                        ACT.Copy).then_inc(uv_ready, 1)

            act.wait_ge(flag_ready, 1)
            is_fast = act.value_load(fast[0:1, 0:1], min_val=0, max_val=1)

            def body(it, first, last):
                for u in range(UN):
                    if has(u, 2, first, last):
                        k = slot(u, 2)
                        for j in range(TILES):
                            act.wait_ge(ot_ready[k][j], count(it, u, 2))
                            if j == 0 and has(u, 3, first, False):
                                act.wait_ge(z_ready[slot(u, 3)], count(it, u, 3))
                            nc.scalar.copy(ot_sb[:, j, :], ot_ps[j][:, :]).then_inc(ot_copied[k][j], 1)
                        act.wait_ge(z_ready[k], count(it, u, 2))
                        if has(u, 4, first, False):
                            act.wait_ge(seg_ready[slot(u, 4)], count(it, u, 4))
                        nc.scalar.activation(t_sb[:, k % 2, :, 0:D],
                                             z_ps[:, 0:TILES * D].rearrange("p (t c) -> p t c", t=TILES),
                                             ACT.Tanh).then_inc(t_ready[k], 1)

            with act.If(is_fast):
                for k in range(UN):
                    act.sem_inc(t_ready[k], 1)
                    for j in range(TILES):
                        act.sem_inc(ot_copied[k][j], 1)
                act.wait_ge(consts, 3)
                windowed(act, body)
            with act.Else():
                act.wait_ge(consts, 3)
                with act.Fori(0, NG) as g:
                    act.wait_ge(g_ot, g + 1)
                    for j in range(TILES):
                        last = nc.scalar.copy(ot_sb[:, j, :], ot_ps[j][:, :])
                    last.then_inc(g_otc, 1)
                    act.wait_ge(g_z, g + 1)
                    nc.scalar.activation(t_sb[:, 0, :, 0:D],
                                         z_ps[:, 0:TILES * D].rearrange("p (t c) -> p t c", t=TILES),
                                         ACT.Tanh).then_inc(g_t, 1)

        @block.vector
        def _(dve):
            x3 = x_sb[:, :].rearrange("p (i d) -> p i d", d=D)
            xc3 = xc.rearrange("p (i d) -> p i d", d=D)
            dve.wait_ge(x_in, 16)
            nc.vector.tensor_reduce(out=stats[:, 0, :], in_=x3, axis=AX.X, op=ALU.add).then_inc(ln, 1)
            dve.wait_ge(ln, 1)
            nc.vector.scalar_tensor_tensor(out=xc3, in0=stats[:, 0, :].unsqueeze(2).to_broadcast([NP, NPP, D]),
                                           scalar=-1.0 / D, in1=x3, op0=ALU.mult, op1=ALU.add).then_inc(ln, 1)
            dve.wait_ge(ln, 2)
            nc.vector.tensor_tensor(xsq, xc, xc, ALU.mult).then_inc(ln, 1)
            dve.wait_ge(ln, 3)
            nc.vector.tensor_reduce(out=stats[:, 3, :], in_=xsq.rearrange("p (i d) -> p i d", d=D), axis=AX.X,
                                    op=ALU.add).then_inc(ln, 1)
            dve.wait_ge(ln, 4)
            nc.vector.tensor_scalar(stats[:, 1, :], stats[:, 3, :], 1.0 / D, EPS, ALU.mult, ALU.add).then_inc(ln, 1)
            dve.wait_ge(wprep_pe, 1)
            dve.wait_ge(weights_in, 16 * N_WEIGHT_DMAS)
            nc.vector.tensor_copy(w2t[:, 0:D], bank[6][0:D, 0:D])
            nc.vector.tensor_copy(wt[:].rearrange("p a d -> p (a d)"), bank[6][0:D, D:3 * D])
            nc.vector.tensor_copy(w3t[:], bank[7][0:D, :]).then_inc(wprep_dve, 1)
            dve.wait_ge(sq_done, 1)
            nc.vector.reciprocal(stats[:, 3, :], stats[:, 2, :]).then_inc(ln, 1)
            dve.wait_ge(ln, 6)
            nc.vector.tensor_tensor(xc3, xc3, stats[:, 3, :].unsqueeze(2).to_broadcast([NP, NPP, D]),
                                    ALU.mult).then_inc(ln, 1)
            dve.wait_ge(wprep_pe, 2)
            nc.vector.tensor_copy(a12[:].rearrange("p a d -> p (a d)"), bank[6][0:D, 0:2 * D]).then_inc(wprep_dve, 1)
            dve.wait_ge(wprep_pe, 3)
            nc.vector.tensor_copy(uvw[:], bank[6][0:D + 1, 128:128 + 2 * D]).then_inc(wprep_dve, 1)
            nc.vector.tensor_copy(g_sb[:].rearrange("p c d -> p (c d)"), bank[7][:, 0:FC * D]).then_inc(wprep_dve, 1)

            dve.wait_ge(rows_in, 96)
            nc.vector.tensor_copy(src_rows, src_raw).then_inc(prep, 1)
            nc.vector.tensor_copy(dst_rows, dst_raw).then_inc(prep, 1)
            dve.wait_ge(prep, 2)
            nc.vector.tensor_reduce(out=rowst[:, 0, :], in_=dst_rows, axis=AX.X, op=ALU.min).then_inc(prep, 1)
            nc.vector.scalar_tensor_tensor(out=loc_rows[:].rearrange("q b j p -> q b (j p)"), in0=dst_rows,
                                           scalar=float(N), in1=dst_rows, op0=ALU.is_lt,
                                           op1=ALU.mult).then_inc(prep, 1)
            dve.wait_ge(prep, 4)
            nc.vector.tensor_reduce(out=rowst[:, 1, :], in_=loc_rows[:].rearrange("q b j p -> q b (j p)"),
                                    axis=AX.X, op=ALU.max).then_inc(prep, 1)
            nc.vector.tensor_scalar(rowst[:, 2, :], rowst[:, 0, :], float(N - W), None, ALU.min).then_inc(prep, 1)
            dve.wait_ge(prep, 6)
            nc.vector.tensor_tensor(rowst[:, 3, :], rowst[:, 1, :], rowst[:, 2, :], ALU.subtract).then_inc(prep, 1)
            for b in range(RB):
                nc.vector.tensor_scalar(loc_rows[:, b, :, :], dst_rows[:, b, :].rearrange("q (p j) -> q j p", j=TILES),
                                        rowst[:, 2, b:b + 1], None, ALU.subtract).then_inc(prep, 1)
            sv = src_e[:, 0:NG * TILES].rearrange("p (g j) -> p g j", j=TILES)
            dv = dst_e[:, :].rearrange("p (g j) -> p g j", j=TILES)
            for k in range(2 * TILES):
                dve.wait_ge(cols_ps, k + 1)
                dest = (sv if k < TILES else dv)[:, :, k % TILES]
                nc.vector.tensor_copy(dest, bank[6 + k % 2][:, 0:NG]).then_inc(cols_read, 1)
            dve.wait_ge(cols_ps, 2 * TILES + 1)
            nc.vector.tensor_reduce(out=span1[:, 0:1], in_=bank[6][0:1, 0:RB * RQ], axis=AX.X,
                                    op=ALU.max).then_inc(cols_read, 1)
            dve.wait_ge(cols_read, 2 * TILES + 1)
            nc.vector.tensor_scalar(fast[:], span1[:, 0:1], float(W), None, ALU.is_lt).then_inc(flag_ready, 1)
            nc.vector.tensor_copy(base_f[:], bank[7][0:1, 0:NG]).then_inc(cols_read, 1)
            nc.vector.tensor_copy(base_row[:], bank[7][0:1, 0:NG]).then_inc(cols_read, 1)
            dve.wait_ge(cols_ps, 2 * TILES + 2)
            nc.vector.tensor_tensor(loc_e[:, :].rearrange("p (g j) -> p g j", j=TILES), dv,
                                    bank[6][:, 0:NG].unsqueeze(2).to_broadcast([P, NG, TILES]),
                                    ALU.subtract).then_inc(cols_read, 1)
            for r in range(3):
                a, b = r % 2, (r + 1) % 2
                nc.vector.tensor_copy(bpart[:], brow[:, a, :]).then_inc(ln, 1)
                dve.wait_ge(ln, 8 + 3 * r)
                q = slice(32 * r, 32 * r + 32)
                nc.vector.tensor_copy(bias_r[q, :].rearrange("q (t c) -> q t c", t=TILES),
                                      bpart[q, :].unsqueeze(1).to_broadcast([32, TILES, D])).then_inc(ln, 1)
                nc.vector.tensor_tensor(brow[:, b, :], brow[:, a, :], bpart[:], ALU.subtract).then_inc(ln, 1)
                dve.wait_ge(ln, 10 + 3 * r)

            dve.wait_ge(consts, 3)
            dve.wait_ge(flag_ready, 1)
            dve.wait_ge(cols_read, 2 * TILES + 4)
            is_fast = dve.value_load(fast[0:1, 0:1], min_val=0, max_val=1)

            def body(it, first, last):
                for u in range(UN):
                    n = it * UN + u
                    if has(u, 4, first, last):
                        k = slot(u, 4)
                        start = dve.value_load(base_row[0:1, bass.ds(n - UN, 1)], min_val=0, max_val=N - W)
                        window = acc[:, bass.ds(start, W)]
                        if has(u, 5, first, False):
                            dve.wait_ge(acc_done[slot(u, 5)], count(it, u, 5))
                        dve.wait_ge(seg_ready[k], count(it, u, 4))
                        nc.vector.tensor_tensor(window, window, seg_ps, ALU.add).then_inc(acc_done[k], 1)
                    if has(u, 1, first, last):
                        k = slot(u, 1)
                        dve.wait_ge(u_in[k], 64 * dma_count(it, u, 1))
                        dve.wait_ge(sv_ready[k], count(it, u, 1))
                        if has(u, 3, first, False):
                            dve.wait_ge(o_ready[slot(u, 3)], count(it, u, 3))
                        nc.vector.tensor_tensor(s_sb[:, k % 2], u_rows[:, k], sv_ps[k % 2],
                                                ALU.add).then_inc(s_ready[k], 1)
                        if not last:
                            nc.vector.tensor_copy(idx_u[:, k, :], src_e[:, bass.ds((n - 1 + UN) * TILES, TILES)]
                                                  ).then_inc(idx_ready[k], 1)
                    if has(u, 0, first, last):
                        dve.wait_ge(loc_in[u], 16 * dma_count(it, u, 0))
                        if has(u, 2, first, False):
                            dve.wait_ge(sv_ready[slot(u, 2)], count(it, u, 2))
                        nc.vector.tensor_scalar(hot_t[:, u % 2, :], loc_bc[0:W, u, :], iota_p[0:W, 0:1], None,
                                                ALU.is_equal).then_inc(hot_t_ready[u], 1)
                        if not first:
                            dve.wait_ge(seg_ready[u], count(it, u, UN))
                        nc.vector.tensor_tensor(
                            hot[:, u, :, :],
                            loc_e[:, bass.ds(n * TILES, TILES)].unsqueeze(2).to_broadcast([P, TILES, W]),
                            iota_f[:, 0:W].unsqueeze(1).to_broadcast([P, TILES, W]),
                            ALU.is_equal).then_inc(hot_ready[u], 1)
                    if has(u, 1, first, last):
                        k = slot(u, 1)
                        if has(u, 3, first, False):
                            dve.wait_ge(ot_ready[slot(u, 3)][TILES - 1], count(it, u, 3))
                        dve.wait_ge(s_ready[k], count(it, u, 1))
                        nc.vector.tensor_tensor(
                            o_sb[:, k % 2], s_sb[:, k % 2].unsqueeze(2).to_broadcast([P, TILES, NB, D]),
                            basis[:, bass.ds((n - 1) * TILES * NB, TILES * NB)].rearrange(
                                "p (t b) -> p t b", t=TILES).unsqueeze(3).to_broadcast([P, TILES, NB, D]),
                            ALU.mult).then_inc(o_ready[k], 1)

            def first_indices():
                for k in range(UN):
                    nc.vector.tensor_copy(idx_u[:, k, :], src_e[:, k * TILES:(k + 1) * TILES]
                                          ).then_inc(idx_ready[k], 1)

            with dve.If(is_fast):
                for k in range(UN):
                    for s in (hot_t_ready, hot_ready, s_ready, o_ready, acc_done):
                        dve.sem_inc(s[k], 1)
                first_indices()
                dve.wait_ge(basis_in[0], 16)
                dve.wait_ge(basis_in[1], 16)
                windowed(dve, body, halves=True)
                for k in range(UN):
                    dve.wait_ge(acc_done[k], ITERS + 1)
            with dve.Else():
                dve.wait_ge(basis_in[0], 16)
                dve.wait_ge(basis_in[1], 16)
                dve.wait_ge(basis_in[2], 32)
                dve.sem_inc(g_seg, 1)
                with dve.Fori(0, NG) as g:
                    nc.vector.tensor_copy(idx_u[:, 0, :], src_e[:, bass.ds(g * TILES, TILES)])
                    nc.vector.tensor_copy(idx_v[:], dst_e[:, bass.ds(g * TILES, TILES)])
                    nc.vector.tensor_copy(dcur[:], dst_e[:, bass.ds(g * TILES, TILES)])
                    dve.drain()
                    nc.vector.tensor_scalar(idx_v[:], idx_v[:], float(N - 1), None, ALU.min).then_inc(g_idx, 1)
                    dve.wait_ge(g_rows, (g + 1) * (2 * TILES * 16))
                    nc.vector.tensor_tensor(s_sb[:, 0], u_rows[:, 0], v_rows[:], ALU.add)
                    dve.drain()
                    nc.vector.tensor_tensor(
                        o_sb[:, 0], s_sb[:, 0].unsqueeze(2).to_broadcast([P, TILES, NB, D]),
                        basis[:, bass.ds(g * TILES * NB, TILES * NB)].rearrange(
                            "p (t b) -> p t b", t=TILES).unsqueeze(3).to_broadcast([P, TILES, NB, D]),
                        ALU.mult).then_inc(g_o, 1)
                    dve.wait_ge(g_ot, g + 1)
                    dve.sem_inc(held, 1)
                    with dve.Fori(0, NBLK) as blk:
                        dve.wait_ge(g_seg, g * NBLK + blk + 1)
                        for j in range(TILES):
                            last = nc.vector.tensor_scalar(hot_blk[:, j, :], iota_f[:], dcur[:, j:j + 1], None,
                                                           ALU.is_equal)
                        last.then_inc(g_hot, 1)
                        dve.drain()
                        nc.vector.tensor_scalar(dcur[:], dcur[:], -float(BW), None, ALU.add)
                        dve.wait_ge(g_seg, g * NBLK + blk + 2)
                        nc.vector.tensor_tensor(acc[:, bass.ds(blk * BW, BW)], acc[:, bass.ds(blk * BW, BW)],
                                                bank[7][0:D + 1, :], ALU.add).then_inc(g_dve, 1)
                        dve.drain()
            dve.drain().then_inc(acc_ready, 1)

            for c in range(7):
                n = min(8, NPP - 8 * c) * D
                dve.wait_ge(y_ps, c + 1)
                nc.vector.tensor_tensor(x_sb[:, c * 512:c * 512 + n], x_sb[:, c * 512:c * 512 + n],
                                        bank[c][0:NP, 0:n], ALU.add).then_inc(y_ready, 1)

        @block.tensor
        def _(pe):
            pe.wait_ge(consts, 2)
            pe.wait_ge(weights_in, 16 * N_WEIGHT_DMAS)
            for k in range(3):
                nc.tensor.transpose(bank[6][0:D, k * D:(k + 1) * D], wraw[:, k, :], ident[0:D, 0:D])
            for b in range(NB):
                last = nc.tensor.transpose(bank[7][0:D, b * D:(b + 1) * D],
                                           w3[:].rearrange("k (c b) -> k b c", b=NB)[:, b, :], ident[0:D, 0:D])
            last.then_inc(wprep_pe, 1)
            pe.wait_ge(wprep_dve, 1)
            for k in range(2):
                last = nc.tensor.matmul(bank[6][0:D, k * D:(k + 1) * D], wt[:, k, :], p2[:], start=True, stop=True)
            last.then_inc(wprep_pe, 1)
            for c in range(FC):
                nc.tensor.matmul(bank[7][:, c * D:(c + 1) * D], w3t[:, c * P:(c + 1) * P], iw1[:], start=True,
                                 stop=True)
            pe.wait_ge(wprep_dve, 2)
            pe.wait_ge(consts, 3)
            nc.tensor.matmul(bank[6][0:D + 1, 128:128 + D], w2t[:], a12[:, 0, :], start=True, stop=True)
            nc.tensor.matmul(bank[6][0:D + 1, 192:192 + D], w2t[:], a12[:, 1, :], start=True, stop=False)
            nc.tensor.matmul(bank[6][0:D + 1, 192:192 + D], c1[:], p2[:], start=False, stop=False)
            nc.tensor.matmul(bank[6][0:D + 1, 192:192 + D], c2[:], b2row[:], start=False, stop=True
                             ).then_inc(wprep_pe, 1)
            pe.wait_ge(ln, 7)
            xc3 = xc.rearrange("p (i d) -> p i d", d=D)

            def columns(k):
                rows = src_rows if k < TILES else dst_rows
                if k >= 2:
                    pe.wait_ge(cols_read, k - 1)
                for b in range(RB):
                    last = nc.tensor.transpose(
                        bank[6 + k % 2][:, b * RQ:(b + 1) * RQ],
                        rows[:, b, :].rearrange("q (p j) -> q j p", j=TILES)[:, k % TILES, :], ident[0:RQ, 0:RQ])
                last.then_inc(cols_ps, 1)

            for c in range(len(CHUNKS) + 2):
                if c < len(CHUNKS):
                    i0, n = CHUNKS[c]
                    if c >= 2:
                        pe.wait_ge(ht_ready, c - 1)
                    for i in range(n):
                        last = nc.tensor.transpose(bank[c % 2][0:D, i * NP:(i + 1) * NP], xc3[:, i0 + i, :],
                                                   ident[0:NP, 0:NP])
                    last.then_inc(ht_ps_ready, 1)
                if 1 <= c <= len(CHUNKS):
                    k = c - 1
                    n = CHUNKS[k][1]
                    pe.wait_ge(ht_ready, k + 1)
                    if k >= 2:
                        pe.wait_ge(a_ready, k - 1)
                    nc.tensor.matmul(bank[2 + k % 2][0:D, 0:n * NP], w1[:], h_t[:, k % 2, 0:n * NP], start=True,
                                     stop=True).then_inc(a_ps_ready, 1)
                if c >= 2:
                    k = c - 2
                    n = CHUNKS[k][1]
                    pe.wait_ge(a_ready, k + 1)
                    pe.wait_ge(wprep_dve, 4)
                    if k >= 2:
                        pe.wait_ge(uv_ready, k - 1)
                    for i in range(n):
                        last = nc.tensor.matmul(bank[4 + k % 2][0:NP, i * 2 * D:(i + 1) * 2 * D],
                                                a_t[:, k % 2, i * NP:(i + 1) * NP], uvw[:], start=True, stop=True)
                    last.then_inc(uv_ps_ready, 1)
                if 7 <= c:
                    if c == 7:
                        pe.wait_ge(prep, 7)
                    columns(c - 7)
            pe.wait_ge(cols_read, 2 * TILES)
            for b in range(RB):
                for row, k in ((3, 6), (2, 7)):
                    last = nc.tensor.transpose(bank[k][0:1, b * RQ:(b + 1) * RQ], rowst[:, row, b:b + 1],
                                               ident[0:RQ, 0:RQ])
            last.then_inc(cols_ps, 1)
            pe.wait_ge(cols_read, 2 * TILES + 3)
            nc.tensor.matmul(bank[6][:, 0:NG], ones1[:], base_f[:], start=True, stop=True).then_inc(cols_ps, 1)

            pe.wait_ge(cols_read, 2 * TILES + 4)
            pe.wait_ge(ln, 16)
            pe.wait_ge(uv_ready, len(CHUNKS))
            pe.wait_ge(flag_ready, 1)
            is_fast = pe.value_load(fast[0:1, 0:1], min_val=0, max_val=1)

            def transposes(o, j):
                for c in range(FC):
                    last = nc.tensor.transpose(ot_ps[j][:, c * P:(c + 1) * P],
                                               o[:, j, 2 * c:2 * c + 2, :].rearrange("p b k -> p (b k)"), ident[:])
                return last

            def z_bias(z):
                nc.tensor.matmul(z[:, 0:TILES * D], bias_l[:], bias_r[:], start=True, stop=False,
                                 skip_group_check=True)

            def z_tile(z, j):
                for c in range(FC):
                    last = nc.tensor.matmul(z[:, j * D:(j + 1) * D], ot_sb[:, j, c * P:(c + 1) * P], g_sb[:, c, :],
                                            start=False, stop=(c == FC - 1), skip_group_check=True)
                return last

            def body(it, first, last_pass):
                for u in range(UN):
                    if has(u, 2, first, last_pass):
                        k = slot(u, 2)
                        pe.wait_ge(o_ready[k], count(it, u, 2))
                        for j in range(TILES):
                            if has(u, 3, first, False):
                                pe.wait_ge(ot_copied[slot(u, 3)][j], count(it, u, 3))
                            transposes(o_sb[:, k % 2], j).then_inc(ot_ready[k][j], 1)
                    if has(u, 0, first, last_pass):
                        pe.wait_ge(v_in[u], 16 * dma_count(it, u, 0))
                        if has(u, 2, first, False):
                            pe.wait_ge(s_ready[slot(u, 2)], count(it, u, 2))
                        pe.wait_ge(hot_t_ready[u], count(it, u, 0))
                        for j in range(TILES):
                            last = nc.tensor.matmul(sv_ps[u % 2][:, j, :], hot_t[:, u % 2, j * P:(j + 1) * P],
                                                    v_win[:, u, :], start=True, stop=True)
                        last.then_inc(sv_ready[u], 1)
                    if has(u, 3, first, last_pass):
                        k = slot(u, 3)
                        pe.wait_ge(t_ready[k], count(it, u, 3))
                        if has(u, 4, first, False):
                            pe.wait_ge(acc_done[slot(u, 4)], count(it, u, 4))
                        pe.wait_ge(hot_ready[k], count(it, u, 3))
                        for j in range(TILES):
                            last = nc.tensor.matmul(seg_ps, t_sb[:, k % 2, j, :], hot[:, k, j, :],
                                                    start=(j == 0), stop=(j == TILES - 1))
                        last.then_inc(seg_ready[k], 1)
                    if has(u, 2, first, last_pass):
                        k = slot(u, 2)
                        if has(u, 3, first, False):
                            pe.wait_ge(t_ready[slot(u, 3)], count(it, u, 3))
                        z_bias(z_ps)
                        for j in range(TILES):
                            pe.wait_ge(ot_copied[k][j], count(it, u, 2))
                            last = z_tile(z_ps, j)
                        last.then_inc(z_ready[k], 1)

            with pe.If(is_fast):
                for k in range(UN):
                    for s in (sv_ready, z_ready, seg_ready):
                        pe.sem_inc(s[k], 1)
                    for j in range(TILES):
                        pe.sem_inc(ot_ready[k][j], 1)
                windowed(pe, body)
            with pe.Else():
                with pe.Fori(0, NG) as g:
                    pe.wait_ge(g_o, g + 1)
                    for j in range(TILES):
                        last = transposes(o_sb[:, 0], j)
                    last.then_inc(g_ot, 1)
                    z_bias(z_ps)
                    pe.wait_ge(g_otc, g + 1)
                    for j in range(TILES):
                        last = z_tile(z_ps, j)
                    last.then_inc(g_z, 1)
                    pe.wait_ge(g_t, g + 1)
                    pe.sem_inc(held, 1)
                    with pe.Fori(0, NBLK) as blk:
                        pe.wait_ge(g_hot, g * NBLK + blk + 1)
                        for j in range(TILES):
                            last = nc.tensor.matmul(bank[7][0:D + 1, :], t_sb[:, 0, j, :], hot_blk[:, j, :],
                                                    start=(j == 0), stop=(j == TILES - 1))
                        last.then_inc(g_seg, 1)

            pe.wait_ge(acc_ready, 1)
            nodes = acc[:, 0:N].rearrange("c (p i) -> c i p", i=NPP)
            for c in range(7):
                for i in range(8 * c, min(8 * c + 8, NPP)):
                    last = nc.tensor.matmul(bank[c][0:NP, (i - 8 * c) * D:(i - 8 * c + 1) * D], nodes[:, i, :],
                                            w_out[:], start=True, stop=True)
                last.then_inc(y_ps, 1)


NAMES = ["x", "src", "dst", "edge_attr_8"] + ["L0_gnn_" + n for n in (
    "pp_W1", "pp_b1", "pp_W2", "pp_b2", "pi_W1", "pi_b1", "pi_W2", "pi_b2", "pi_W3", "ii_W1", "ii_b1", "ii_W2",
    "ii_b2")]


def kernel(**inputs):
    import concourse.bacc as bacc
    from concourse.bass_utils import run_bass_kernel_spmd

    nc = bacc.Bacc("TRN2", target_bir_lowering=False, num_devices=1)
    arrays = {n: np.ascontiguousarray(inputs[n]) for n in NAMES}
    aps = [nc.dram_tensor(n, arrays[n].shape, mybir.dt.from_np(arrays[n].dtype), kind="ExternalInput").ap()
           for n in NAMES]
    n_nodes, d = arrays["x"].shape
    f32 = mybir.dt.float32
    out = nc.dram_tensor("out", (n_nodes, d), f32, kind="ExternalOutput").ap()
    u_tab = nc.dram_tensor("u_tab", (n_nodes, d), f32).ap()
    v_tab = nc.dram_tensor("v_tab", (n_nodes, d), f32).ap()
    loc_tab = nc.dram_tensor("loc_tab", (392, 512), f32).ap()
    program(nc, *aps, out, u_tab, v_tab, loc_tab)
    r = run_bass_kernel_spmd(nc, [arrays], core_ids=[0])
    return r.results[0]["out"]
```

```python
from contextlib import ExitStack

import numpy as np

import concourse.bass as bass
from concourse import mybir


def program(nc, x, src, dst, edge_attr, pp_W1, pp_b1, pp_W2, pp_b2, pi_W1, pi_b1, pi_W2, pi_b2, pi_W3,
            ii_W1, ii_b1, ii_W2, ii_b2, out, u_tab, vf_tab, v_tab, loc_tab):
    f32, i32, u32, bf16 = mybir.dt.float32, mybir.dt.int32, mybir.dt.uint32, mybir.dt.bfloat16
    ALU, ACT, AX = mybir.AluOpType, mybir.ActivationFunctionType, mybir.AxisListType

    N, D = x.shape
    E, NB = edge_attr.shape
    P = 128
    EPS = 1e-5

    NPP = 50
    NP = N // NPP
    CH = 4
    CHUNKS = [(c, min(CH, NPP - c)) for c in range(0, NPP, CH)]

    TILES = 4
    GE = P * TILES
    UN = 4
    NG = -(-E // (GE * UN)) * UN
    ITERS = NG // UN
    FULL = E // GE
    PART = (E - FULL * GE) // TILES
    RB = 4
    RQ = NG // RB
    W = 64
    BW = 512
    NBLK = -(-N // BW)
    F = NB * D
    FC = F // P
    SPLIT_IT = ITERS // 2 - 1
    SPLIT = UN * (SPLIT_IT + 1)
    EARLY = 4 * UN

    assert NP * NPP == N and RQ * RB == NG and RQ <= P and PART * TILES + FULL * GE == E and F == FC * P

    ctx = ExitStack()
    with ctx:
        def sb(name, shape, dt=f32):
            return ctx.enter_context(nc.sbuf_tensor(name, shape, dt))

        def sem(name):
            return ctx.enter_context(nc.semaphore(name))

        def sems(name, n):
            return [sem(f"{name}{i}") for i in range(n)]

        x_sb = sb("x_sb", [NP, NPP * D])
        basis = sb("basis", [P, NG * TILES * NB])
        src_e = sb("src_e", [P, (NG + UN) * TILES], i32)
        dst_e = sb("dst_e", [P, NG * TILES])
        loc_e = sb("loc_e", [P, NG * TILES])
        base_row = sb("base_row", [1, NG], i32)
        acc_full = sb("acc_full", [P, NBLK * BW])
        acc = acc_full[0:D + 1, :]
        ident = sb("ident", [P, P])
        iota_f = sb("iota_f", [P, BW])
        iota_p = sb("iota_p", [P, 1])
        g_sb = sb("g_sb", [P, FC, D])
        w_out = sb("w_out", [D + 1, D])
        z_bias = sb("z_bias", [P, 1])
        fast = sb("fast", [1, 1], i32)

        idx_u = sb("idx_u", [P, UN, TILES], i32)
        idx_v = sb("idx_v", [P, TILES], i32)
        u_rows = sb("u_rows", [P, UN, TILES, D])
        v_rows = sb("v_rows", [P, TILES, D])
        v_win = sb("v_win", [P, UN, 2, D], bf16)
        loc_bc = sb("loc_bc", [P, UN, GE], bf16)
        hot_t = sb("hot_t", [P, 2, GE], bf16)
        hot = sb("hot", [P, UN, TILES, W])
        s_sb = sb("s_sb", [P, 2, TILES, D])
        o_sb = sb("o_sb", [P, 2, TILES, NB, D])
        ot_sb = sb("ot_sb", [P, FC, TILES, P])
        tt_sb = sb("tt_sb", [P, 2, 2 * P])
        t_sb = sb("t_sb", [P, 2, TILES, D + 1])
        dcur = sb("dcur", [P, TILES])

        w1 = sb("w1", [D, D])
        p2 = sb("p2", [D, D])
        iw1 = sb("iw1", [D, D])
        wraw = sb("wraw", [D, 3, D])
        w3 = sb("w3", [D, D * NB])
        wt = sb("wt", [D, 2, D])
        w2t = sb("w2t", [D, D + 1])
        a12 = sb("a12", [D, 2, D])
        w3t = sb("w3t", [D, F])
        c1 = sb("c1", [D, D + 1])
        c2 = sb("c2", [1, D + 1])
        b2row = sb("b2row", [1, D])
        b1col = sb("b1col", [D, 1])
        uvw = sb("uvw", [D + 1, 2 * D])
        stats = sb("stats", [NP, 4, NPP])
        h_t = sb("h_t", [D, 2, CH * NP])
        a_t = sb("a_t", [D + 1, 2, CH * NP])
        uv_sb = sb("uv_sb", [NP, 2, 2, CH, D])
        v_parts = sb("v_parts", [NP, 2, CH, 3, D], bf16)
        v_rest = sb("v_rest", [NP, 2, CH, D])
        rowst = sb("rowst", [RQ, 4, RB])
        span1 = sb("span1", [1, 2])
        base_f = sb("base_f", [1, NG])
        ones1 = sb("ones1", [1, P])
        loc_rows = sb("loc_rows", [RQ, RB, TILES, P], bf16)
        dst_cut = sb("dst_cut", [RQ, RB, GE])
        dst_rows = sb("dst_rows", [RQ, RB, GE])
        xc = o_sb[0:NP, :, :, :, :].rearrange("p a t b k -> p (a t b k)")[:, 0:NPP * D]
        src_rows = ot_sb[0:RQ, :, :, :].rearrange("q c t e -> q c (t e)")
        src_raw = src_rows.bitcast(i32)
        dst_raw = dst_rows[:, :, :].bitcast(i32)
        xsq = acc_full[0:NP, 0:NPP * D]
        hot_blk = o_sb[:, 0, :, :, :].rearrange("p t b k -> p t (b k)")

        bank = [ctx.enter_context(nc.psum_tensor(f"bank{i}", [P, 512], f32)) for i in range(8)]
        ot_ps = bank[0:4]
        sv_ps = bank[4][:, 0:TILES * D].rearrange("p (t k) -> p t k", t=TILES)
        z_ps = bank[5]
        tt_ps = bank[6]
        seg_ps = bank[7][0:D + 1, 0:W]

        x_in = sem("x_in")
        weights_in = sem("weights_in")
        padded = sem("padded")
        consts = sem("consts")
        rows_in = sem("rows_in")
        basis_in = sems("basis_in", 3)
        ln = sem("ln")
        sq_done = sem("sq_done")
        prep = sem("prep")
        wprep_pe = sem("wprep_pe")
        wprep_dve = sem("wprep_dve")
        ht_ps_ready = sem("ht_ps_ready")
        ht_ready = sem("ht_ready")
        a_ps_ready = sem("a_ps_ready")
        a_ready = sem("a_ready")
        uv_ps_ready = sem("uv_ps_ready")
        uv_ready = sem("uv_ready")
        v_split = sem("v_split")
        v_part = sem("v_part")
        tables_out = [sem(f"tables_out{i}") for i in range(2)]
        loc_out = sem("loc_out")
        cols_ps = sem("cols_ps")
        cols_read = sem("cols_read")
        flag_ready = sem("flag_ready")
        zeroed = sem("zeroed")
        held = sem("held")

        idx_ready = sems("idx_ready", UN)
        u_in = sems("u_in", UN)
        v_in = sems("v_in", UN)
        loc_in = sems("loc_in", UN)
        hot_t_ready = sems("hot_t_ready", UN)
        hot_ready = sems("hot_ready", UN)
        sv_ready = sems("sv_ready", UN)
        s_ready = sems("s_ready", UN)
        o_ready = sems("o_ready", UN)
        ot_ready = [sems(f"ot_ready{k}_", TILES) for k in range(UN)]
        ot_copied = [sems(f"ot_copied{k}_", TILES) for k in range(UN)]
        z_ready = sems("z_ready", UN)
        tt_ready = sems("tt_ready", UN)
        t_ps_ready = sems("t_ps_ready", UN)
        t_ready = sems("t_ready", UN)
        seg_ready = sems("seg_ready", UN)
        acc_done = sems("acc_done", UN)

        g_idx = sem("g_idx")
        g_rows = sem("g_rows")
        g_o = sem("g_o")
        g_ot = sem("g_ot")
        g_otc = sem("g_otc")
        g_z = sem("g_z")
        g_tt = sem("g_tt")
        g_tps = sem("g_tps")
        g_t = sem("g_t")
        g_hot = sem("g_hot")
        g_seg = sem("g_seg")
        g_dve = sem("g_dve")

        acc_ready = sem("acc_ready")
        y_ps = sem("y_ps")
        y_ready = sem("y_ready")
        stored = sem("stored")

        block = ctx.enter_context(nc.Block())

        def slot(u, lag):
            return (u - lag) % UN

        def count(it, u, lag):
            return it + 2 + (u - lag) // UN

        def dma_count(it, u, lag):
            return it + 1 + (u - lag) // UN

        def has(u, lag, first, last):
            return (not first or u >= lag) and (not last or u < lag)

        def windowed(eng, body, halves=False):
            body(0, True, False)
            if halves:
                with eng.Fori(1, SPLIT_IT) as it:
                    body(it, False, False)
                eng.wait_ge(basis_in[2], 32)
                with eng.Fori(SPLIT_IT, ITERS) as it:
                    body(it, False, False)
            else:
                with eng.Fori(1, ITERS) as it:
                    body(it, False, False)
            body(ITERS, False, True)

        N_TAB = [16 * len(CHUNKS[i::2]) * 3 for i in range(2)]
        N_WEIGHT_DMAS = 15

        @block.sync
        def _(sp):
            xv = x.rearrange("(p i) d -> p (i d)", i=NPP)
            sp.dma_start(x_sb[:, :], xv).then_inc(x_in, 16)
            sp.wait_ge(padded, 1)
            for raw, idx in ((src_raw, src), (dst_raw, dst)):
                whole = (RB - 1) * RQ
                sp.dma_start(raw[:, 0:RB - 1, :], idx[0:whole * GE].rearrange(
                    "(b q e) -> q b e", b=RB - 1, e=GE)).then_inc(rows_in, 16)
                sp.dma_start(raw[0:FULL - whole, RB - 1, :], idx[whole * GE:FULL * GE].rearrange(
                    "(q e) -> q e", e=GE)).then_inc(rows_in, 16)
                sp.dma_start(raw[FULL - whole:FULL - whole + 1, RB - 1, 0:E - FULL * GE],
                             idx[FULL * GE:E].rearrange("(q e) -> q e", q=1)).then_inc(rows_in, 16)
            bv = basis[:, :].rearrange("p (g f) -> p g f", g=NG)
            for (lo, hi), done in zip(((0, EARLY), (EARLY, SPLIT), (SPLIT, FULL)), basis_in):
                sp.dma_start(bv[:, lo:hi, :], edge_attr[lo * GE:hi * GE, :].rearrange(
                    "(g p j) b -> p g (j b)", p=P, j=TILES)).then_inc(done, 16)
            sp.dma_start(bv[0:PART, FULL, :], edge_attr[FULL * GE:E, :].rearrange(
                "(p j) b -> p (j b)", j=TILES)).then_inc(basis_in[2], 16)
            sp.wait_ge(prep, 11)
            sp.dma_start(loc_tab.rearrange("(b q) e -> q b e", b=RB),
                         loc_rows[:, :, :, :].rearrange("q b j p -> q b (j p)")).then_inc(loc_out, 16)
            u_v = u_tab.rearrange("(p i) d -> p i d", i=NPP)
            vf_v = vf_tab.rearrange("(p i) d -> p i d", i=NPP)
            v_v = v_tab.rearrange("(p i) w d -> p i (w d)", i=NPP)
            for c, (i0, n) in enumerate(CHUNKS):
                sp.wait_ge(uv_ready, c + 1)
                sp.dma_start(u_v[:, i0:i0 + n, :], uv_sb[:, c % 2, 0, 0:n, :]).then_inc(tables_out[c % 2], 16)
                sp.dma_start(vf_v[:, i0:i0 + n, :], uv_sb[:, c % 2, 1, 0:n, :]).then_inc(tables_out[c % 2], 16)
                sp.wait_ge(v_split, c + 1)
                sp.dma_start(v_v[:, i0:i0 + n, :], v_parts[:, c % 2, 0:n, :, :].rearrange("p i w d -> p i (w d)")
                             ).then_inc(tables_out[c % 2], 16)

            sp.wait_ge(tables_out[0], N_TAB[0])
            sp.wait_ge(tables_out[1], N_TAB[1])
            sp.wait_ge(loc_out, 16)
            sp.wait_ge(cols_read, 2 * TILES + 3)
            sp.wait_ge(flag_ready, 1)
            is_fast = sp.value_load(fast[0:1, 0:1], min_val=0, max_val=1)

            def body(it, first, last):
                for u in range(UN):
                    if has(u, 0, first, last):
                        start = sp.value_load(base_row[0:1, bass.ds(it * UN + u, 1)], min_val=0, max_val=N - W)
                        if not first:
                            sp.wait_ge(hot_t_ready[u], count(it, u, UN))
                        sp.dma_start(loc_bc[:, u, :], loc_tab[bass.ds(it * UN + u, 1), :].to_broadcast(
                            [P, GE])).then_inc(loc_in[u], 16)
                        if not first:
                            sp.wait_ge(sv_ready[u], count(it, u, UN))
                        sp.dma_start(v_win[0:W, u, :, :], v_tab[bass.ds(start, W), 0:2, :]).then_inc(v_in[u], 16)
                        sp.dma_start(v_win[W:P, u, 0, :], v_tab[bass.ds(start, W), 2, :]).then_inc(v_in[u], 16)

            with sp.If(is_fast):
                windowed(sp, body)

            ov = out.rearrange("(p i) d -> p (i d)", i=NPP)
            half = 24 * D
            sp.wait_ge(y_ready, 3)
            sp.dma_start(ov[:, 0:half], x_sb[:, 0:half]).then_inc(stored, 16)
            sp.wait_ge(y_ready, 7)
            sp.dma_start(ov[:, half:], x_sb[:, half:]).then_inc(stored, 16)
            sp.wait_ge(stored, 32)

        @block.gpsimd
        def _(pool):
            nc.gpsimd.memset(src_raw[:, RB - 1, :], 0)
            nc.gpsimd.memset(dst_raw[:, RB - 1, :], N)
            nc.gpsimd.memset(basis[:, FULL * TILES * NB:], 0.0)
            pool.drain().then_inc(padded, 1)
            nc.gpsimd.memset(ident[:], 0.0).then_inc(zeroed, 1)
            pool.wait_ge(zeroed, 1)
            nc.gpsimd.affine_select(out=ident[:], in_=ident[:], compare_op=ALU.not_equal, fill=1.0, base=0,
                                    pattern=[[-1, P]], channel_multiplier=1).then_inc(consts, 1)
            nc.gpsimd.memset(c1[:], 0.0)
            nc.gpsimd.memset(c2[:], 0.0)
            nc.gpsimd.memset(ones1[:], 1.0)
            nc.gpsimd.memset(a_t[:], 1.0)
            pool.drain().then_inc(consts, 1)
            nc.gpsimd.memset(c2[:, D:D + 1], 1.0)
            nc.gpsimd.iota(iota_f[:], pattern=[[1, BW]], base=0, channel_multiplier=0,
                           allow_small_or_imprecise_dtypes=True)
            nc.gpsimd.iota(iota_p[0:W, :], pattern=[[0, 1]], base=0, channel_multiplier=1,
                           allow_small_or_imprecise_dtypes=True)
            nc.gpsimd.memset(v_win[:], 0.0)
            pool.drain().then_inc(zeroed, 1)
            pool.wait_ge(zeroed, 2)
            nc.gpsimd.iota(iota_p[W:P, :], pattern=[[0, 1]], base=0, channel_multiplier=1,
                           allow_small_or_imprecise_dtypes=True).then_inc(zeroed, 1)
            pool.wait_ge(zeroed, 3)
            nc.gpsimd.memset(t_sb[:], 1.0)
            pool.wait_ge(ln, 4)
            nc.gpsimd.memset(acc, 0.0)
            nc.gpsimd.memset(src_e[:, NG * TILES:], 0)
            pool.drain().then_inc(consts, 1)

            pool.wait_ge(tables_out[0], N_TAB[0])
            pool.wait_ge(tables_out[1], N_TAB[1])
            pool.wait_ge(flag_ready, 1)
            is_fast = pool.value_load(fast[0:1, 0:1], min_val=0, max_val=1)

            def body(it, first, last):
                for u in range(UN):
                    if has(u, 0, first, last):
                        pool.wait_ge(idx_ready[u], dma_count(it, u, 0))
                        if not first:
                            pool.wait_ge(s_ready[u], count(it, u, UN))
                        pool.sem_inc(held, 1)
                        for j in range(TILES):
                            pool.indirect_dma_start(
                                out=u_rows[:, u, j, :], out_offset=None, in_=u_tab[:, :],
                                in_offset=bass.IndirectOffsetOnAxis(ap=idx_u[:, u, j:j + 1].bitcast(u32), axis=0),
                            ).then_inc(u_in[u], 16)

            with pool.If(is_fast):
                windowed(pool, body)
            with pool.Else():
                with pool.Fori(0, NG) as g:
                    pool.wait_ge(g_idx, g + 1)
                    pool.sem_inc(held, 1)
                    for j in range(TILES):
                        for rows, tab, idx in ((u_rows[:, 0], u_tab, idx_u[:, 0]), (v_rows, vf_tab, idx_v)):
                            pool.indirect_dma_start(
                                out=rows[:, j, :], out_offset=None, in_=tab[:, :],
                                in_offset=bass.IndirectOffsetOnAxis(ap=idx[:, j:j + 1].bitcast(u32), axis=0),
                            ).then_inc(g_rows, 16)

        @block.scalar
        def _(act):
            loads = [(wraw[:, 0, :], pp_W2), (wraw[:, 1, :], pi_W1[0:D, :]), (wraw[:, 2, :], pi_W1[D:2 * D, :]),
                     (p2[:], pi_W2), (w1[:], pp_W1), (b1col[:], pp_b1.rearrange("(p a) -> p a", a=1)),
                     (w2t[:, D:D + 1], pp_b2.rearrange("(p a) -> p a", a=1)),
                     (b2row[:], pi_b2.rearrange("(a d) -> a d", a=1)),
                     (w3[:], pi_W3), (iw1[:], ii_W1), (w_out[0:D, :], ii_W2),
                     (w_out[D:D + 1, :], ii_b2.rearrange("(a d) -> a d", a=1))]
            for dest, source in loads:
                act.dma_start(dest, source).then_inc(weights_in, 16)
            act.wait_ge(consts, 2)
            act.dma_start(c1[:, D:D + 1], pi_b1.rearrange("(p a) -> p a", a=1)).then_inc(weights_in, 16)
            for r in range(2):
                act.dma_start(z_bias[r * D:(r + 1) * D, :], ii_b1.rearrange("(p a) -> p a", a=1)).then_inc(
                    weights_in, 16)

            act.wait_ge(ln, 5)
            nc.scalar.activation(stats[:, 2, :], stats[:, 1, :], ACT.Sqrt).then_inc(sq_done, 1)

            for c in range(len(CHUNKS) + 2):
                if c < len(CHUNKS):
                    i0, n = CHUNKS[c]
                    act.wait_ge(ht_ps_ready, c + 1)
                    if c >= 2:
                        act.wait_ge(a_ps_ready, c - 1)
                    nc.scalar.activation(h_t[:, c % 2, 0:n * NP], bank[c % 2][0:D, 0:n * NP],
                                         ACT.Relu).then_inc(ht_ready, 1)
                if 1 <= c <= len(CHUNKS):
                    k = c - 1
                    i0, n = CHUNKS[k]
                    act.wait_ge(a_ps_ready, k + 1)
                    act.wait_ge(weights_in, 16 * N_WEIGHT_DMAS)
                    if k >= 2:
                        act.wait_ge(uv_ps_ready, k - 1)
                    nc.scalar.activation(a_t[0:D, k % 2, 0:n * NP], bank[2 + k % 2][0:D, 0:n * NP], ACT.Tanh,
                                         bias=b1col[:, 0:1]).then_inc(a_ready, 1)
                if c >= 2:
                    k = c - 2
                    i0, n = CHUNKS[k]
                    act.wait_ge(uv_ps_ready, k + 1)
                    if k >= 2:
                        act.wait_ge(tables_out[k % 2], 48 * (k // 2))
                    nc.scalar.activation(
                        uv_sb[:, k % 2, :, 0:n, :].rearrange("p w i d -> p i w d"),
                        bank[4 + k % 2][0:NP, 0:n * 2 * D].rearrange("p (i w d) -> p i w d", w=2, d=D),
                        ACT.Copy).then_inc(uv_ready, 1)

            act.wait_ge(flag_ready, 1)
            is_fast = act.value_load(fast[0:1, 0:1], min_val=0, max_val=1)

            def tanh_z(r):
                return nc.scalar.activation(tt_sb[:, r, :], z_ps[:, 0:2 * P], ACT.Tanh, bias=z_bias[:, 0:1])

            def copy_ot(j):
                return nc.scalar.copy(ot_sb[:, :, j, :], ot_ps[j][:, :].rearrange("p (c e) -> p c e", c=FC))

            def copy_t(r):
                return nc.scalar.copy(t_sb[:, r, :, 0:D].rearrange("p (h q) c -> p q h c", h=2),
                                      tt_ps[:, 0:TILES * D].rearrange("p (q h c) -> p q h c", q=2, h=2))

            def body(it, first, last):
                for u in range(UN):
                    if has(u, 3, first, last):
                        k = slot(u, 3)
                        act.wait_ge(z_ready[k], count(it, u, 3))
                        if has(u, 5, first, False):
                            act.wait_ge(t_ps_ready[slot(u, 5)], count(it, u, 5))
                        tanh_z(k % 2).then_inc(tt_ready[k], 1)
                    if has(u, 2, first, last):
                        k = slot(u, 2)
                        if has(u, 3, first, False):
                            act.wait_ge(z_ready[slot(u, 3)], count(it, u, 3))
                        for j in range(TILES):
                            act.wait_ge(ot_ready[k][j], count(it, u, 2))
                            copy_ot(j).then_inc(ot_copied[k][j], 1)
                    if has(u, 3, first, last):
                        k = slot(u, 3)
                        act.wait_ge(t_ps_ready[k], count(it, u, 3))
                        if has(u, 5, first, False):
                            act.wait_ge(seg_ready[slot(u, 5)], count(it, u, 5))
                        copy_t(k % 2).then_inc(t_ready[k], 1)

            with act.If(is_fast):
                for k in range(UN):
                    act.sem_inc(t_ready[k], 1)
                    act.sem_inc(tt_ready[k], 1)
                    for j in range(TILES):
                        act.sem_inc(ot_copied[k][j], 1)
                act.wait_ge(consts, 3)
                windowed(act, body)
            with act.Else():
                act.wait_ge(consts, 3)
                with act.Fori(0, NG) as g:
                    act.wait_ge(g_ot, g + 1)
                    for j in range(TILES):
                        last = copy_ot(j)
                    last.then_inc(g_otc, 1)
                    act.wait_ge(g_z, g + 1)
                    tanh_z(0).then_inc(g_tt, 1)
                    act.wait_ge(g_tps, g + 1)
                    copy_t(0).then_inc(g_t, 1)

        @block.vector
        def _(dve):
            x3 = x_sb[:, :].rearrange("p (i d) -> p i d", d=D)
            xc3 = xc.rearrange("p (i d) -> p i d", d=D)
            dve.wait_ge(x_in, 16)
            nc.vector.tensor_reduce(out=stats[:, 0, :], in_=x3, axis=AX.X, op=ALU.add).then_inc(ln, 1)
            dve.wait_ge(ln, 1)
            nc.vector.scalar_tensor_tensor(out=xc3, in0=stats[:, 0, :].unsqueeze(2).to_broadcast([NP, NPP, D]),
                                           scalar=-1.0 / D, in1=x3, op0=ALU.mult, op1=ALU.add).then_inc(ln, 1)
            dve.wait_ge(ln, 2)
            nc.vector.tensor_tensor(xsq, xc, xc, ALU.mult).then_inc(ln, 1)
            dve.wait_ge(ln, 3)
            nc.vector.tensor_reduce(out=stats[:, 3, :], in_=xsq.rearrange("p (i d) -> p i d", d=D), axis=AX.X,
                                    op=ALU.add).then_inc(ln, 1)
            dve.wait_ge(ln, 4)
            nc.vector.tensor_scalar(stats[:, 1, :], stats[:, 3, :], 1.0 / D, EPS, ALU.mult, ALU.add).then_inc(ln, 1)
            dve.wait_ge(wprep_pe, 1)
            dve.wait_ge(weights_in, 16 * N_WEIGHT_DMAS)
            nc.vector.tensor_copy(w2t[:, 0:D], bank[6][0:D, 0:D])
            nc.vector.tensor_copy(wt[:].rearrange("p a d -> p (a d)"), bank[6][0:D, D:3 * D])
            nc.vector.tensor_copy(w3t[:], bank[7][0:D, :]).then_inc(wprep_dve, 1)
            dve.wait_ge(sq_done, 1)
            nc.vector.reciprocal(stats[:, 3, :], stats[:, 2, :]).then_inc(ln, 1)
            dve.wait_ge(ln, 6)
            nc.vector.tensor_tensor(xc3, xc3, stats[:, 3, :].unsqueeze(2).to_broadcast([NP, NPP, D]),
                                    ALU.mult).then_inc(ln, 1)
            dve.wait_ge(wprep_pe, 2)
            nc.vector.tensor_copy(a12[:].rearrange("p a d -> p (a d)"), bank[6][0:D, 0:2 * D]).then_inc(wprep_dve, 1)
            dve.wait_ge(wprep_pe, 3)
            nc.vector.tensor_copy(uvw[:], bank[6][0:D + 1, 128:128 + 2 * D]).then_inc(wprep_dve, 1)
            nc.vector.tensor_copy(g_sb[:].rearrange("p c d -> p (c d)"), bank[7][:, 0:FC * D]).then_inc(wprep_dve, 1)

            part_count = [0]

            def split_v(chunks):
                for c in chunks:
                    n = CHUNKS[c][1]
                    v, rest, parts = uv_sb[:, c % 2, 1, 0:n, :], v_rest[:, c % 2, 0:n, :], v_parts[:, c % 2, 0:n]
                    dve.wait_ge(uv_ready, c + 1)
                    if c >= 2:
                        dve.wait_ge(tables_out[c % 2], 48 * (c // 2))
                    nc.vector.tensor_copy(parts[:, :, 0, :], v).then_inc(v_part, 1)
                    dve.wait_ge(v_part, part_count[0] + 1)
                    nc.vector.tensor_tensor(rest, v, parts[:, :, 0, :], ALU.subtract).then_inc(v_part, 1)
                    dve.wait_ge(v_part, part_count[0] + 2)
                    nc.vector.tensor_copy(parts[:, :, 2, :], rest).then_inc(v_part, 1)
                    dve.wait_ge(v_part, part_count[0] + 3)
                    nc.vector.tensor_tensor(parts[:, :, 1, :], rest, parts[:, :, 2, :],
                                            ALU.subtract).then_inc(v_split, 1)
                    part_count[0] += 3

            dve.wait_ge(rows_in, 96)
            nc.vector.tensor_copy(src_rows, src_raw).then_inc(prep, 1)
            nc.vector.tensor_copy(dst_rows[:], dst_raw).then_inc(prep, 1)
            dve.wait_ge(prep, 2)
            nc.vector.tensor_reduce(out=rowst[:, 0, :], in_=dst_rows[:], axis=AX.X, op=ALU.min).then_inc(prep, 1)
            nc.vector.scalar_tensor_tensor(out=dst_cut[:], in0=dst_rows[:], scalar=float(N), in1=dst_rows[:],
                                           op0=ALU.is_lt, op1=ALU.mult).then_inc(prep, 1)
            dve.wait_ge(prep, 4)
            nc.vector.tensor_reduce(out=rowst[:, 1, :], in_=dst_cut[:], axis=AX.X, op=ALU.max).then_inc(prep, 1)
            nc.vector.tensor_scalar(rowst[:, 2, :], rowst[:, 0, :], float(N - W), None, ALU.min).then_inc(prep, 1)
            dve.wait_ge(prep, 6)
            nc.vector.tensor_tensor(rowst[:, 3, :], rowst[:, 1, :], rowst[:, 2, :], ALU.subtract).then_inc(prep, 1)
            for b in range(RB):
                nc.vector.tensor_scalar(loc_rows[:, b, :, :], dst_rows[:, b, :].rearrange("q (p j) -> q j p", j=TILES),
                                        rowst[:, 2, b:b + 1], None, ALU.subtract).then_inc(prep, 1)
            split_v(range(0, 5))
            sv = src_e[:, 0:NG * TILES].rearrange("p (g j) -> p g j", j=TILES)
            dv = dst_e[:, :].rearrange("p (g j) -> p g j", j=TILES)
            for k in range(2 * TILES):
                split_v(range(5 + k, 6 + k))
                dve.wait_ge(cols_ps, k + 1)
                dest = (sv if k < TILES else dv)[:, :, k % TILES]
                nc.vector.tensor_copy(dest, bank[6 + k % 2][:, 0:NG]).then_inc(cols_read, 1)
            dve.wait_ge(cols_ps, 2 * TILES + 1)
            nc.vector.tensor_reduce(out=span1[:, 0:1], in_=bank[6][0:1, 0:RB * RQ], axis=AX.X,
                                    op=ALU.max).then_inc(cols_read, 1)
            dve.wait_ge(cols_read, 2 * TILES + 1)
            nc.vector.tensor_scalar(fast[:], span1[:, 0:1], float(W), None, ALU.is_lt).then_inc(flag_ready, 1)
            nc.vector.tensor_copy(base_f[:], bank[7][0:1, 0:NG]).then_inc(cols_read, 1)
            nc.vector.tensor_copy(base_row[:], bank[7][0:1, 0:NG]).then_inc(cols_read, 1)
            dve.wait_ge(cols_ps, 2 * TILES + 2)
            nc.vector.tensor_tensor(loc_e[:, :].rearrange("p (g j) -> p g j", j=TILES), dv,
                                    bank[6][:, 0:NG].unsqueeze(2).to_broadcast([P, NG, TILES]),
                                    ALU.subtract).then_inc(cols_read, 1)
            dve.wait_ge(consts, 3)
            dve.wait_ge(flag_ready, 1)
            dve.wait_ge(cols_read, 2 * TILES + 4)
            is_fast = dve.value_load(fast[0:1, 0:1], min_val=0, max_val=1)

            def body(it, first, last):
                for u in range(UN):
                    n = it * UN + u
                    if has(u, 1, first, last):
                        k = slot(u, 1)
                        dve.wait_ge(u_in[k], 64 * dma_count(it, u, 1))
                        dve.wait_ge(sv_ready[k], count(it, u, 1))
                        if has(u, 3, first, False):
                            dve.wait_ge(o_ready[slot(u, 3)], count(it, u, 3))
                        nc.vector.tensor_tensor(s_sb[:, k % 2], u_rows[:, k], sv_ps,
                                                ALU.add).then_inc(s_ready[k], 1)
                        if not last:
                            nc.vector.tensor_copy(idx_u[:, k, :], src_e[:, bass.ds((n - 1 + UN) * TILES, TILES)]
                                                  ).then_inc(idx_ready[k], 1)
                    if has(u, 0, first, last):
                        dve.wait_ge(loc_in[u], 16 * dma_count(it, u, 0))
                        if has(u, 2, first, False):
                            dve.wait_ge(sv_ready[slot(u, 2)], count(it, u, 2))
                        nc.vector.tensor_scalar(hot_t[:, u % 2, :], loc_bc[:, u, :], iota_p[:, 0:1], None,
                                                ALU.is_equal).then_inc(hot_t_ready[u], 1)
                    if has(u, 2, first, last):
                        k = slot(u, 2)
                        if has(u, 6, first, False):
                            dve.wait_ge(seg_ready[k], count(it, u, 6))
                        nc.vector.tensor_tensor(
                            hot[:, k, :, :],
                            loc_e[:, bass.ds((n - 2) * TILES, TILES)].unsqueeze(2).to_broadcast([P, TILES, W]),
                            iota_f[:, 0:W].unsqueeze(1).to_broadcast([P, TILES, W]),
                            ALU.is_equal).then_inc(hot_ready[k], 1)
                    if has(u, 1, first, last):
                        k = slot(u, 1)
                        if has(u, 3, first, False):
                            dve.wait_ge(ot_ready[slot(u, 3)][TILES - 1], count(it, u, 3))
                        dve.wait_ge(s_ready[k], count(it, u, 1))
                        nc.vector.tensor_tensor(
                            o_sb[:, k % 2], s_sb[:, k % 2].unsqueeze(2).to_broadcast([P, TILES, NB, D]),
                            basis[:, bass.ds((n - 1) * TILES * NB, TILES * NB)].rearrange(
                                "p (t b) -> p t b", t=TILES).unsqueeze(3).to_broadcast([P, TILES, NB, D]),
                            ALU.mult).then_inc(o_ready[k], 1)
                    if has(u, 4, first, last):
                        k = slot(u, 4)
                        start = dve.value_load(base_row[0:1, bass.ds(n - UN, 1)], min_val=0, max_val=N - W)
                        window = acc[:, bass.ds(start, W)]
                        if has(u, 5, first, False):
                            dve.wait_ge(acc_done[slot(u, 5)], count(it, u, 5))
                        dve.wait_ge(seg_ready[k], count(it, u, 4))
                        nc.vector.tensor_tensor(window, window, seg_ps, ALU.add).then_inc(acc_done[k], 1)

            def first_indices():
                for k in range(UN):
                    nc.vector.tensor_copy(idx_u[:, k, :], src_e[:, k * TILES:(k + 1) * TILES]
                                          ).then_inc(idx_ready[k], 1)

            with dve.If(is_fast):
                for k in range(UN):
                    for s in (hot_t_ready, hot_ready, s_ready, o_ready, acc_done):
                        dve.sem_inc(s[k], 1)
                first_indices()
                dve.wait_ge(basis_in[0], 16)
                dve.wait_ge(basis_in[1], 16)
                windowed(dve, body, halves=True)
                for k in range(UN):
                    dve.wait_ge(acc_done[k], ITERS + 1)
            with dve.Else():
                dve.wait_ge(basis_in[0], 16)
                dve.wait_ge(basis_in[1], 16)
                dve.wait_ge(basis_in[2], 32)
                dve.sem_inc(g_seg, 1)
                with dve.Fori(0, NG) as g:
                    nc.vector.tensor_copy(idx_u[:, 0, :], src_e[:, bass.ds(g * TILES, TILES)])
                    nc.vector.tensor_copy(idx_v[:], dst_e[:, bass.ds(g * TILES, TILES)])
                    nc.vector.tensor_copy(dcur[:], dst_e[:, bass.ds(g * TILES, TILES)])
                    dve.drain()
                    nc.vector.tensor_scalar(idx_v[:], idx_v[:], float(N - 1), None, ALU.min).then_inc(g_idx, 1)
                    dve.wait_ge(g_rows, (g + 1) * (2 * TILES * 16))
                    nc.vector.tensor_tensor(s_sb[:, 0], u_rows[:, 0], v_rows[:], ALU.add)
                    dve.drain()
                    nc.vector.tensor_tensor(
                        o_sb[:, 0], s_sb[:, 0].unsqueeze(2).to_broadcast([P, TILES, NB, D]),
                        basis[:, bass.ds(g * TILES * NB, TILES * NB)].rearrange(
                            "p (t b) -> p t b", t=TILES).unsqueeze(3).to_broadcast([P, TILES, NB, D]),
                        ALU.mult).then_inc(g_o, 1)
                    dve.wait_ge(g_ot, g + 1)
                    dve.sem_inc(held, 1)
                    with dve.Fori(0, NBLK) as blk:
                        dve.wait_ge(g_seg, g * NBLK + blk + 1)
                        for j in range(TILES):
                            last = nc.vector.tensor_scalar(hot_blk[:, j, :], iota_f[:], dcur[:, j:j + 1], None,
                                                           ALU.is_equal)
                        last.then_inc(g_hot, 1)
                        dve.drain()
                        nc.vector.tensor_scalar(dcur[:], dcur[:], -float(BW), None, ALU.add)
                        dve.wait_ge(g_seg, g * NBLK + blk + 2)
                        nc.vector.tensor_tensor(acc[:, bass.ds(blk * BW, BW)], acc[:, bass.ds(blk * BW, BW)],
                                                bank[7][0:D + 1, :], ALU.add).then_inc(g_dve, 1)
                        dve.drain()
            dve.drain().then_inc(acc_ready, 1)

            for c in range(7):
                n = min(8, NPP - 8 * c) * D
                dve.wait_ge(y_ps, c + 1)
                nc.vector.tensor_tensor(x_sb[:, c * 512:c * 512 + n], x_sb[:, c * 512:c * 512 + n],
                                        bank[c][0:NP, 0:n], ALU.add).then_inc(y_ready, 1)

        @block.tensor
        def _(pe):
            pe.wait_ge(consts, 2)
            pe.wait_ge(weights_in, 16 * N_WEIGHT_DMAS)
            for k in range(3):
                nc.tensor.transpose(bank[6][0:D, k * D:(k + 1) * D], wraw[:, k, :], ident[0:D, 0:D])
            for b in range(NB):
                last = nc.tensor.transpose(bank[7][0:D, b * D:(b + 1) * D],
                                           w3[:].rearrange("k (c b) -> k b c", b=NB)[:, b, :], ident[0:D, 0:D])
            last.then_inc(wprep_pe, 1)
            pe.wait_ge(wprep_dve, 1)
            for k in range(2):
                last = nc.tensor.matmul(bank[6][0:D, k * D:(k + 1) * D], wt[:, k, :], p2[:], start=True, stop=True)
            last.then_inc(wprep_pe, 1)
            for c in range(FC):
                nc.tensor.matmul(bank[7][:, c * D:(c + 1) * D], w3t[:, c * P:(c + 1) * P], iw1[:], start=True,
                                 stop=True)
            pe.wait_ge(wprep_dve, 2)
            pe.wait_ge(consts, 3)
            nc.tensor.matmul(bank[6][0:D + 1, 128:128 + D], w2t[:], a12[:, 0, :], start=True, stop=True)
            nc.tensor.matmul(bank[6][0:D + 1, 192:192 + D], w2t[:], a12[:, 1, :], start=True, stop=False)
            nc.tensor.matmul(bank[6][0:D + 1, 192:192 + D], c1[:], p2[:], start=False, stop=False)
            nc.tensor.matmul(bank[6][0:D + 1, 192:192 + D], c2[:], b2row[:], start=False, stop=True
                             ).then_inc(wprep_pe, 1)
            pe.wait_ge(ln, 7)
            xc3 = xc.rearrange("p (i d) -> p i d", d=D)

            def columns(k):
                rows = src_rows if k < TILES else dst_rows
                if k >= 2:
                    pe.wait_ge(cols_read, k - 1)
                for b in range(RB):
                    last = nc.tensor.transpose(
                        bank[6 + k % 2][:, b * RQ:(b + 1) * RQ],
                        rows[:, b, :].rearrange("q (p j) -> q j p", j=TILES)[:, k % TILES, :], ident[0:RQ, 0:RQ])
                last.then_inc(cols_ps, 1)

            for c in range(len(CHUNKS) + 2):
                if c < len(CHUNKS):
                    i0, n = CHUNKS[c]
                    if c >= 2:
                        pe.wait_ge(ht_ready, c - 1)
                    for i in range(n):
                        last = nc.tensor.transpose(bank[c % 2][0:D, i * NP:(i + 1) * NP], xc3[:, i0 + i, :],
                                                   ident[0:NP, 0:NP])
                    last.then_inc(ht_ps_ready, 1)
                if 1 <= c <= len(CHUNKS):
                    k = c - 1
                    n = CHUNKS[k][1]
                    pe.wait_ge(ht_ready, k + 1)
                    if k >= 2:
                        pe.wait_ge(a_ready, k - 1)
                    nc.tensor.matmul(bank[2 + k % 2][0:D, 0:n * NP], w1[:], h_t[:, k % 2, 0:n * NP], start=True,
                                     stop=True).then_inc(a_ps_ready, 1)
                if c >= 2:
                    k = c - 2
                    n = CHUNKS[k][1]
                    pe.wait_ge(a_ready, k + 1)
                    pe.wait_ge(wprep_dve, 4)
                    if k >= 2:
                        pe.wait_ge(uv_ready, k - 1)
                    for i in range(n):
                        last = nc.tensor.matmul(bank[4 + k % 2][0:NP, i * 2 * D:(i + 1) * 2 * D],
                                                a_t[:, k % 2, i * NP:(i + 1) * NP], uvw[:], start=True, stop=True)
                    last.then_inc(uv_ps_ready, 1)
                if 7 <= c:
                    if c == 7:
                        pe.wait_ge(prep, 7)
                    columns(c - 7)
            pe.wait_ge(cols_read, 2 * TILES)
            for b in range(RB):
                for row, k in ((3, 6), (2, 7)):
                    last = nc.tensor.transpose(bank[k][0:1, b * RQ:(b + 1) * RQ], rowst[:, row, b:b + 1],
                                               ident[0:RQ, 0:RQ])
            last.then_inc(cols_ps, 1)
            pe.wait_ge(cols_read, 2 * TILES + 3)
            nc.tensor.matmul(bank[6][:, 0:NG], ones1[:], base_f[:], start=True, stop=True).then_inc(cols_ps, 1)

            pe.wait_ge(cols_read, 2 * TILES + 4)
            pe.wait_ge(uv_ready, len(CHUNKS))
            pe.wait_ge(flag_ready, 1)
            is_fast = pe.value_load(fast[0:1, 0:1], min_val=0, max_val=1)

            def transposes(o, j):
                for c in range(FC):
                    last = nc.tensor.transpose(ot_ps[j][:, c * P:(c + 1) * P],
                                               o[:, j, 2 * c:2 * c + 2, :].rearrange("p b k -> p (b k)"), ident[:])
                return last

            def z_group():
                for c in range(FC):
                    for h in range(2):
                        last = nc.tensor.matmul(z_ps[h * D:(h + 1) * D, 0:2 * P], g_sb[:, c, :],
                                                ot_sb[:, c, 2 * h:2 * h + 2, :].rearrange("p t e -> p (t e)"),
                                                start=(c == 0), stop=(c == FC - 1))
                return last

            def t_transposes(r):
                for q in range(2):
                    last = nc.tensor.transpose(tt_ps[:, q * P:(q + 1) * P], tt_sb[:, r, q * P:(q + 1) * P], ident[:])
                return last

            def body(it, first, last_pass):
                for u in range(UN):
                    if has(u, 2, first, last_pass):
                        k = slot(u, 2)
                        pe.wait_ge(o_ready[k], count(it, u, 2))
                        for j in range(TILES):
                            if has(u, 3, first, False):
                                pe.wait_ge(ot_copied[slot(u, 3)][j], count(it, u, 3))
                            transposes(o_sb[:, k % 2], j).then_inc(ot_ready[k][j], 1)
                    if has(u, 3, first, last_pass):
                        k = slot(u, 3)
                        pe.wait_ge(tt_ready[k], count(it, u, 3))
                        if has(u, 4, first, False):
                            pe.wait_ge(t_ready[slot(u, 4)], count(it, u, 4))
                        t_transposes(k % 2).then_inc(t_ps_ready[k], 1)
                    if has(u, 0, first, last_pass):
                        pe.wait_ge(v_in[u], 32 * dma_count(it, u, 0))
                        if has(u, 1, first, False):
                            pe.wait_ge(s_ready[slot(u, 1)], count(it, u, 1))
                        pe.wait_ge(hot_t_ready[u], count(it, u, 0))
                        for j in range(TILES):
                            for w in range(2):
                                last = nc.tensor.matmul(sv_ps[:, j, :], hot_t[:, u % 2, j * P:(j + 1) * P],
                                                        v_win[:, u, w, :], start=(w == 0), stop=(w == 1))
                        last.then_inc(sv_ready[u], 1)
                    if has(u, 4, first, last_pass):
                        k = slot(u, 4)
                        pe.wait_ge(t_ready[k], count(it, u, 4))
                        if has(u, 5, first, False):
                            pe.wait_ge(acc_done[slot(u, 5)], count(it, u, 5))
                        pe.wait_ge(hot_ready[k], count(it, u, 4))
                        for j in range(TILES):
                            last = nc.tensor.matmul(seg_ps, t_sb[:, k % 2, j, :], hot[:, k, j, :],
                                                    start=(j == 0), stop=(j == TILES - 1))
                        last.then_inc(seg_ready[k], 1)
                    if has(u, 2, first, last_pass):
                        k = slot(u, 2)
                        for j in range(TILES):
                            pe.wait_ge(ot_copied[k][j], count(it, u, 2))
                        if has(u, 3, first, False):
                            pe.wait_ge(tt_ready[slot(u, 3)], count(it, u, 3))
                        z_group().then_inc(z_ready[k], 1)

            with pe.If(is_fast):
                for k in range(UN):
                    for s in (sv_ready, z_ready, t_ps_ready, seg_ready):
                        pe.sem_inc(s[k], 1)
                    for j in range(TILES):
                        pe.sem_inc(ot_ready[k][j], 1)
                windowed(pe, body)
            with pe.Else():
                with pe.Fori(0, NG) as g:
                    pe.wait_ge(g_o, g + 1)
                    for j in range(TILES):
                        last = transposes(o_sb[:, 0], j)
                    last.then_inc(g_ot, 1)
                    pe.wait_ge(g_otc, g + 1)
                    z_group().then_inc(g_z, 1)
                    pe.wait_ge(g_tt, g + 1)
                    t_transposes(0).then_inc(g_tps, 1)
                    pe.wait_ge(g_t, g + 1)
                    pe.sem_inc(held, 1)
                    with pe.Fori(0, NBLK) as blk:
                        pe.wait_ge(g_hot, g * NBLK + blk + 1)
                        for j in range(TILES):
                            last = nc.tensor.matmul(bank[7][0:D + 1, :], t_sb[:, 0, j, :], hot_blk[:, j, :],
                                                    start=(j == 0), stop=(j == TILES - 1))
                        last.then_inc(g_seg, 1)

            pe.wait_ge(acc_ready, 1)
            nodes = acc[:, 0:N].rearrange("c (p i) -> c i p", i=NPP)
            for c in range(7):
                for i in range(8 * c, min(8 * c + 8, NPP)):
                    last = nc.tensor.matmul(bank[c][0:NP, (i - 8 * c) * D:(i - 8 * c + 1) * D], nodes[:, i, :],
                                            w_out[:], start=True, stop=True)
                last.then_inc(y_ps, 1)


NAMES = ["x", "src", "dst", "edge_attr_8"] + ["L0_gnn_" + n for n in (
    "pp_W1", "pp_b1", "pp_W2", "pp_b2", "pi_W1", "pi_b1", "pi_W2", "pi_b2", "pi_W3", "ii_W1", "ii_b1", "ii_W2",
    "ii_b2")]


def kernel(**inputs):
    import concourse.bacc as bacc
    from concourse.bass_utils import run_bass_kernel_spmd

    nc = bacc.Bacc("TRN2", target_bir_lowering=False, num_devices=1)
    arrays = {n: np.ascontiguousarray(inputs[n]) for n in NAMES}
    aps = [nc.dram_tensor(n, arrays[n].shape, mybir.dt.from_np(arrays[n].dtype), kind="ExternalInput").ap()
           for n in NAMES]
    n_nodes, d = arrays["x"].shape
    f32 = mybir.dt.float32
    out = nc.dram_tensor("out", (n_nodes, d), f32, kind="ExternalOutput").ap()
    u_tab = nc.dram_tensor("u_tab", (n_nodes, d), f32).ap()
    vf_tab = nc.dram_tensor("vf_tab", (n_nodes, d), f32).ap()
    v_tab = nc.dram_tensor("v_tab", (n_nodes, 3, d), mybir.dt.bfloat16).ap()
    loc_tab = nc.dram_tensor("loc_tab", (392, 512), mybir.dt.bfloat16).ap()
    program(nc, *aps, out, u_tab, vf_tab, v_tab, loc_tab)
    r = run_bass_kernel_spmd(nc, [arrays], core_ids=[0])
    return r.results[0]["out"]
```

```python
from contextlib import ExitStack

import numpy as np

import concourse.bass as bass
from concourse import mybir


def program(nc, x, src, dst, edge_attr, pp_W1, pp_b1, pp_W2, pp_b2, pi_W1, pi_b1, pi_W2, pi_b2, pi_W3,
            ii_W1, ii_b1, ii_W2, ii_b2, out, u_tab, v_tab, loc_tab):
    f32, i32, u32, bf16 = mybir.dt.float32, mybir.dt.int32, mybir.dt.uint32, mybir.dt.bfloat16
    ALU, ACT, AX = mybir.AluOpType, mybir.ActivationFunctionType, mybir.AxisListType

    N, D = x.shape
    E, NB = edge_attr.shape
    P = 128
    EPS = 1e-5

    NPP = 50
    NP = N // NPP
    PAIRS = NPP // 2
    CHUNKS = [(q, min(4, PAIRS - q)) for q in range(0, PAIRS, 4)]
    HALVES = [(q, min(2, PAIRS - q)) for q in range(0, PAIRS, 2)]
    C_STARTS = 6
    HPC = 2

    TILES = 4
    GE = P * TILES
    UN = 4
    NG = -(-E // (GE * UN)) * UN
    ITERS = NG // UN
    FULL = E // GE
    PART = (E - FULL * GE) // TILES
    RB = 4
    RQ = NG // RB
    W = P // 3
    BW = 512
    NBLK = -(-N // BW)
    F = NB * D
    FC = F // P
    NBT = TILES * NB
    QT = P // TILES
    AHEAD = 2
    NR = 4
    PIECE = next(n for n in range(15, FULL + 1) if FULL % n == 0)
    EARLY = 9
    LATE = FULL // PIECE - EARLY
    NEED = (EARLY * PIECE - AHEAD) // UN

    assert NP * NPP == N and RQ * RB == NG and RQ <= P and PART * TILES + FULL * GE == E and F == FC * P
    assert LATE + 2 < NEED < ITERS
    assert 3 * NB <= QT and 2 * D == P

    ctx = ExitStack()
    with ctx:
        def sb(name, shape, dt=f32):
            return ctx.enter_context(nc.sbuf_tensor(name, shape, dt))

        def sem(name):
            return ctx.enter_context(nc.semaphore(name))

        def sems(name, n):
            return [sem(f"{name}{i}") for i in range(n)]

        x_sb = sb("x_sb", [NP, NPP * D])
        basis = sb("basis", [P, (NG + AHEAD) * NBT])
        src_e = sb("src_e", [P, (NG + UN) * TILES], i32)
        dst_e = sb("dst_e", [P, NG * TILES])
        loc_e = sb("loc_e", [P, NG * TILES])
        base_row = sb("base_row", [1, NG], i32)
        acc = sb("acc", [D + 1, NBLK * BW])
        ident = sb("ident", [P, P])
        ident_b = sb("ident_b", [P, P], bf16)
        iota_f = sb("iota_f", [P, BW])
        iota_i = sb("iota_i", [P, 2], i32)
        iota_p = sb("iota_p", [P, 3])
        iota_8 = sb("iota_8", [P, 1])
        spread = sb("spread", [P, NB, D], bf16)
        g_sb = sb("g_sb", [P, FC, D])
        w_out = sb("w_out", [D + 1, D])
        z_bias = sb("z_bias", [P, 1])
        s_bias = sb("s_bias", [P, 1])
        fast = sb("fast", [1, 1], i32)

        idx_u = sb("idx_u", [P, UN, TILES], i32)
        idx_v = sb("idx_v", [P, TILES], i32)
        u_rows = sb("u_rows", [P, UN, TILES, D])
        v_rows = sb("v_rows", [P, TILES, 3, D], bf16)
        v_win = sb("v_win", [3 * W, UN, D], bf16)
        loc_bc = sb("loc_bc", [3 * W, UN, GE], bf16)
        hot_t = sb("hot_t", [3 * W, 2, GE], bf16)
        hot = sb("hot", [P, UN, TILES, W])
        s_sb = sb("s_sb", [P, TILES, D])
        st_sb = sb("st_sb", [P, 4, GE])
        b_parts = sb("b_parts", [P, UN, TILES, QT], bf16)
        b_rest = sb("b_rest", [P, 2, 2 * NBT])
        bt_sb = sb("bt_sb", [P, 2, P], bf16)
        o_sb = sb("o_sb", [P, 2, FC, GE])
        tt_sb = sb("tt_sb", [P, 2, 2 * P])
        t_sb = sb("t_sb", [P, 2, TILES, D + 1])
        dcur = sb("dcur", [P, TILES])
        ut_sb = st_sb[:, 0:2, :]
        s2_sb = st_sb[:, 2:4, :]

        w1 = sb("w1", [P, P])
        b1col = sb("b1col", [P, 1])
        p2 = sb("p2", [D, D])
        iw1 = sb("iw1", [D, D])
        wraw = sb("wraw", [D, 3, D])
        w3 = sb("w3", [D, D * NB])
        wt = sb("wt", [D, 3, D])
        a12 = sb("a12", [D, 2, D])
        w3t = sb("w3t", [D, F])
        b2col = sb("b2col", [D, 1])
        pb1col = sb("pb1col", [D, 1])
        b2row = sb("b2row", [1, D])
        uvw = sb("uvw", [P, 2, P])
        stats = sb("stats", [NP, 6, NPP])
        h_t = sb("h_t", [P, 2, 4 * NP])
        a_t = sb("a_t", [P, 2, 4 * NP])
        v_parts = sb("v_parts", [NP, NR, 4, 3, D], bf16)
        u_out = u_rows[0:NP, 0:NR, 0:4, :]
        v_rest = tt_sb[0:NP, :, :].rearrange("p r (i d) -> p r i d", d=D)
        rowst = sb("rowst", [RQ, 4, RB])
        span1 = sb("span1", [1, 1])
        base_f = sb("base_f", [1, NG])
        ones1 = sb("ones1", [1, P])
        loc_rows = sb("loc_rows", [RQ, RB, TILES, P], bf16)
        src_rows = sb("src_rows", [RQ, RB, GE])
        dst_rows = sb("dst_rows", [RQ, RB, GE])
        src_raw = src_rows[:, :, :].bitcast(i32)
        dst_raw = dst_rows[:, :, :].bitcast(i32)
        dst_cut = st_sb[0:RQ, :, :]
        node_area = o_sb[0:NP, :, :, :].rearrange("p a c e -> p (a c e)")
        xn = node_area[:, 0:NPP * D].rearrange("p (i d) -> p i d", d=D)
        bn = node_area[:, NPP * D:NPP * (D + 6)].rearrange("p (i s) -> p i s", s=6)
        src_gj = src_e[:, 0:NG * TILES].rearrange("p (g j) -> p g j", j=TILES)
        dst_gj = dst_e[:, :].rearrange("p (g j) -> p g j", j=TILES)
        hot_blk = o_sb[:, 1, :, :]

        spread_ps = ctx.enter_context(nc.psum_tensor("spread_ps", [P, TILES, FC * P], f32))
        bank = [spread_ps[:, i, :] for i in range(TILES)] + [
            ctx.enter_context(nc.psum_tensor(f"bank{i}", [P, 512], f32))[:, :] for i in range(TILES, 8)]
        vt_ps = bank[4]
        ut_ps, bt_ps = bank[5][:, 0:2 * P], bank[5][:, 2 * P:3 * P]
        z_ps, t_ps = bank[6][:, 0:2 * P], bank[6][:, 2 * P:2 * P + TILES * D]
        seg_ps = bank[7][0:D + 1, 0:W]

        x_in = sems("x_in", 2)
        weights_in = sem("weights_in")
        more_weights_in = sem("more_weights_in")
        padded = sem("padded")
        zeroed = sem("zeroed")
        consts = sem("consts")
        rows_in = sem("rows_in")
        rows_f = sem("rows_f")
        basis_in = sem("basis_in")
        late_basis_in = sem("late_basis_in")
        ln = sem("ln")
        sq_done = sem("sq_done")
        normed_v = sem("normed_v")
        prep = sem("prep")
        wprep_pe = sem("wprep_pe")
        wprep_act = sem("wprep_act")
        spread_made = sem("spread_made")
        loc_made = sem("loc_made")
        ht_ps_ready = sem("ht_ps_ready")
        ht_ready = sem("ht_ready")
        a_ps_ready = sem("a_ps_ready")
        a_ready = sem("a_ready")
        uv_ps_ready = sem("uv_ps_ready")
        v_first = sem("v_first")
        v_rested = sem("v_rested")
        uv_ready = sem("uv_ready")
        v_split = sem("v_split")
        u_out_done = sems("u_out_done", NR)
        v_out_done = sems("v_out_done", NR)
        loc_out = sem("loc_out")
        cols_ps = sem("cols_ps")
        cols_read = sem("cols_read")
        starts_ps = sem("starts_ps")
        starts_read = sem("starts_read")
        flag_ready = sem("flag_ready")
        held = sem("held")

        idx_ready = sems("idx_ready", UN)
        u_in = sems("u_in", UN)
        v_in = sems("v_in", UN)
        loc_in = sems("loc_in", UN)
        hot_t_ready = sems("hot_t_ready", UN)
        hot_ready = sems("hot_ready", UN)
        vt_ready = sems("vt_ready", UN)
        ut_ps_ready = sems("ut_ps_ready", UN)
        ut_ready = sems("ut_ready", UN)
        s2_ready = sems("s2_ready", UN)
        part1 = sems("part1_", UN)
        rest = sems("rest", UN)
        part2 = sems("part2_", UN)
        part3 = sems("part3_", UN)
        bt_ps_ready = sems("bt_ps_ready", UN)
        bt_ready = sems("bt_ready", UN)
        spread_ready = sems("spread_ready", UN)
        o_ready = sems("o_ready", UN)
        z_ready = sems("z_ready", UN)
        tt_ready = sems("tt_ready", UN)
        t_ps_ready = sems("t_ps_ready", UN)
        t_ready = sems("t_ready", UN)
        seg_ready = sems("seg_ready", UN)
        acc_done = sems("acc_done", UN)

        g_idx = sem("g_idx")
        g_rows = sem("g_rows")
        g_s = sem("g_s")
        g_parts = sem("g_parts")
        g_ps = sem("g_ps")
        g_st = sem("g_st")
        g_spread = sem("g_spread")
        g_o = sem("g_o")
        g_z = sem("g_z")
        g_tt = sem("g_tt")
        g_tps = sem("g_tps")
        g_t = sem("g_t")
        g_hot = sem("g_hot")
        g_seg = sem("g_seg")

        acc_ready = sem("acc_ready")
        y_ps = sem("y_ps")
        y_ready = sem("y_ready")
        stored = sem("stored")

        block = ctx.enter_context(nc.Block())

        def slot(u, lag):
            return (u - lag) % UN

        def count(it, u, lag):
            return it + 2 + (u - lag) // UN

        def dma_count(it, u, lag):
            return it + 1 + (u - lag) // UN

        def has(u, lag, first, last):
            return (not first or u >= lag) and (not last or u < lag)

        N_TAB = [16 * len(HALVES[i::NR]) for i in range(NR)]
        N_WEIGHTS, N_MORE_WEIGHTS = 8, 6

        @block.sync
        def _(sp):
            xv = x.rearrange("(p i) d -> p (i d)", i=NPP)
            for h in range(2):
                cols = slice(h * NPP // 2 * D, (h + 1) * NPP // 2 * D)
                sp.dma_start(x_sb[:, cols], xv[:, cols]).then_inc(x_in[h], 16)
            sp.wait_ge(padded, 1)
            for raw, idx in ((dst_raw, dst), (src_raw, src)):
                whole = (RB - 1) * RQ
                sp.dma_start(raw[:, 0:RB - 1, :], idx[0:whole * GE].rearrange(
                    "(b q e) -> q b e", b=RB - 1, e=GE)).then_inc(rows_in, 16)
                sp.dma_start(raw[0:FULL - whole, RB - 1, :], idx[whole * GE:FULL * GE].rearrange(
                    "(q e) -> q e", e=GE)).then_inc(rows_in, 16)
                sp.dma_start(raw[FULL - whole:FULL - whole + 1, RB - 1, 0:E - FULL * GE],
                             idx[FULL * GE:E].rearrange("(q e) -> q e", q=1)).then_inc(rows_in, 16)
            bv = basis[:, :].rearrange("p (g f) -> p g f", f=NBT)

            edges = edge_attr[0:FULL * GE, :].rearrange("(g p j) b -> p g (j b)", p=P, j=TILES)

            def load_basis(lo, arrived):
                sp.dma_start(bv[:, bass.ds(lo, PIECE), :], edges[:, bass.ds(lo, PIECE), :]).then_inc(arrived, 16)

            def load_last_basis():
                sp.dma_start(bv[0:PART, FULL, :], edge_attr[FULL * GE:E, :].rearrange(
                    "(p j) b -> p (j b)", j=TILES)).then_inc(late_basis_in, 16)

            sp.wait_ge(more_weights_in, 16 * N_MORE_WEIGHTS)
            for k in range(EARLY):
                load_basis(k * PIECE, basis_in)
            u_v = u_tab.rearrange("(p i) d -> p i d", i=NPP)
            v_v = v_tab.rearrange("(p i) w d -> p i (w d)", i=NPP)
            for h, (q0, n) in enumerate(HALVES):
                sp.wait_ge(uv_ready, h + 1)
                sp.dma_start(u_v[:, 2 * q0:2 * (q0 + n), :], u_out[:, h % NR, 0:2 * n, :]).then_inc(
                    u_out_done[h % NR], 16)
                sp.wait_ge(v_split, h + 1)
                sp.dma_start(v_v[:, 2 * q0:2 * (q0 + n), :],
                             v_parts[:, h % NR, 0:2 * n, :, :].rearrange("p i w d -> p i (w d)")
                             ).then_inc(v_out_done[h % NR], 16)
                if h == len(HALVES) // 2:
                    sp.wait_ge(loc_made, 1)
                    sp.dma_start(loc_tab.rearrange("(b q) e -> q b e", b=RB),
                                 loc_rows[:, :, :, :].rearrange("q b j p -> q b (j p)")).then_inc(loc_out, 16)
            sp.wait_ge(flag_ready, 1)
            is_fast = sp.value_load(fast[0:1, 0:1], min_val=0, max_val=1)
            sp.wait_ge(starts_read, 3)

            for i in range(NR):
                sp.wait_ge(v_out_done[i], N_TAB[i])
                sp.wait_ge(u_out_done[i], N_TAB[i])
            sp.wait_ge(loc_out, 16)

            def body(it, first, last):
                for u in range(UN):
                    if has(u, 0, first, last):
                        start = sp.value_load(base_row[0:1, bass.ds(it * UN + u, 1)], min_val=0, max_val=N - W)
                        if not first:
                            sp.wait_ge(hot_t_ready[u], count(it, u, UN))
                        sp.dma_start(loc_bc[:, u, :], loc_tab[bass.ds(it * UN + u, 1), :].to_broadcast(
                            [3 * W, GE])).then_inc(loc_in[u], 16)
                        if not first:
                            sp.wait_ge(vt_ready[u], count(it, u, UN))
                        sp.dma_start(v_win[:, u, :], v_tab[bass.ds(start, W), :, :].rearrange("n w d -> w n d")
                                     ).then_inc(v_in[u], 16)

            with sp.If(is_fast):
                body(0, True, False)
                load_last_basis()
                with sp.Fori(1, 1 + LATE) as it:
                    body(it, False, False)
                    load_basis((EARLY - 1 + it) * PIECE, late_basis_in)
                with sp.Fori(1 + LATE, ITERS) as it:
                    body(it, False, False)
            with sp.Else():
                load_last_basis()
                with sp.Fori(EARLY, EARLY + LATE) as k:
                    load_basis(k * PIECE, late_basis_in)

            ov = out.rearrange("(p i) d -> p (i d)", i=NPP)
            cuts = [0, 3, 6, 7]
            for lo, hi in zip(cuts, cuts[1:]):
                cols = slice(lo * 8 * D, min(hi * 8, NPP) * D)
                sp.wait_ge(y_ready, hi)
                sp.dma_start(ov[:, cols], x_sb[:, cols]).then_inc(stored, 16)
            sp.wait_ge(stored, 48)

        @block.gpsimd
        def _(pool):
            nc.gpsimd.memset(w1[:], 0.0)
            nc.gpsimd.memset(src_raw[:, RB - 1, :], 0)
            nc.gpsimd.memset(dst_raw[:, RB - 1, :], N)
            nc.gpsimd.memset(basis[:, FULL * NBT:], 0.0)
            pool.drain().then_inc(padded, 1)
            nc.gpsimd.memset(ident[:], 0.0).then_inc(zeroed, 1)
            pool.wait_ge(zeroed, 1)
            nc.gpsimd.affine_select(out=ident[:], in_=ident[:], compare_op=ALU.not_equal, fill=1.0, base=0,
                                    pattern=[[-1, P]], channel_multiplier=1).then_inc(consts, 1)
            nc.gpsimd.memset(ones1[:], 1.0)
            nc.gpsimd.memset(uvw[:], 0.0)
            nc.gpsimd.iota(iota_i[:, 0:1], pattern=[[0, 1]], base=0, channel_multiplier=1)
            pool.drain().then_inc(consts, 1)
            nc.gpsimd.iota(iota_f[:], pattern=[[1, BW]], base=0, channel_multiplier=0,
                           allow_small_or_imprecise_dtypes=True)
            nc.gpsimd.memset(b_parts[:], 0.0)
            nc.gpsimd.memset(t_sb[:], 1.0)
            nc.gpsimd.memset(src_e[:, NG * TILES:], 0)
            nc.gpsimd.memset(acc[:], 0.0)
            pool.drain().then_inc(consts, 1)
            pool.wait_ge(rows_in, 96)
            nc.gpsimd.tensor_copy(dst_rows[:, :, :], dst_raw).then_inc(rows_f, 1)
            nc.gpsimd.tensor_copy(src_rows[:, :, :], src_raw).then_inc(rows_f, 1)
            pool.wait_ge(prep, 2)
            for b in range(RB):
                nc.gpsimd.tensor_scalar(loc_rows[:, b, :, :], dst_rows[:, b, :].rearrange("q (p j) -> q j p", j=TILES),
                                        rowst[:, 2, b:b + 1], None, ALU.subtract)
            pool.drain().then_inc(loc_made, 1)

            pool.wait_ge(flag_ready, 1)
            is_fast = pool.value_load(fast[0:1, 0:1], min_val=0, max_val=1)
            for i in range(NR):
                pool.wait_ge(u_out_done[i], N_TAB[i])

            def body(it, first, last):
                for u in range(UN):
                    if has(u, 0, first, last):
                        pool.wait_ge(idx_ready[u], dma_count(it, u, 0))
                        if not first:
                            pool.wait_ge(ut_ps_ready[u], count(it, u, UN))
                        pool.sem_inc(held, 1)
                        for j in range(TILES):
                            pool.indirect_dma_start(
                                out=u_rows[:, u, j, :], out_offset=None, in_=u_tab[:, :],
                                in_offset=bass.IndirectOffsetOnAxis(ap=idx_u[:, u, j:j + 1].bitcast(u32), axis=0),
                            ).then_inc(u_in[u], 16)

            with pool.If(is_fast):
                body(0, True, False)
                with pool.Fori(1, ITERS) as it:
                    body(it, False, False)
            with pool.Else():
                for i in range(NR):
                    pool.wait_ge(v_out_done[i], N_TAB[i])
                v_lines = v_tab.rearrange("n w d -> n (w d)")
                with pool.Fori(0, NG) as g:
                    pool.wait_ge(g_idx, g + 1)
                    pool.sem_inc(held, 1)
                    for j in range(TILES):
                        pool.indirect_dma_start(
                            out=u_rows[:, 0, j, :], out_offset=None, in_=u_tab[:, :],
                            in_offset=bass.IndirectOffsetOnAxis(ap=idx_u[:, 0, j:j + 1].bitcast(u32), axis=0),
                        ).then_inc(g_rows, 16)
                        pool.indirect_dma_start(
                            out=v_rows[:, j, :, :].rearrange("p w d -> p (w d)"), out_offset=None, in_=v_lines,
                            in_offset=bass.IndirectOffsetOnAxis(ap=idx_v[:, j:j + 1].bitcast(u32), axis=0),
                        ).then_inc(g_rows, 16)

        @block.scalar
        def _(act):
            col = lambda v: v.rearrange("(p a) -> p a", a=1)
            row = lambda v: v.rearrange("(a d) -> a d", a=1)
            twice = lambda v: v.rearrange("(a p c) -> a p c", a=1, c=1).to_broadcast([2, D, 1])
            for dest, source in [
                (wraw[:, 0, :], pp_W2), (wraw[:, 1:3, :], pi_W1.rearrange("(h k) d -> k h d", h=2)),
                (w3[:], pi_W3), (p2[:], pi_W2), (iw1[:], ii_W1), (b2col[:], col(pp_b2)), (pb1col[:], col(pi_b1)),
                (b2row[:], row(pi_b2)),
            ]:
                act.dma_start(dest, source).then_inc(weights_in, 16)
            act.wait_ge(padded, 1)
            for dest, source in [
                (w1[0:D, 0:D], pp_W1), (w1[D:P, D:P], pp_W1), (b1col[:], twice(pp_b1)),
                (w_out[0:D, :], ii_W2), (w_out[D:D + 1, :], row(ii_b2)), (z_bias[:], twice(ii_b1)),
            ]:
                act.dma_start(dest, source).then_inc(more_weights_in, 16)

            act.wait_ge(ln, 5)
            nc.scalar.activation(stats[:, 4, :], stats[:, 3, :], ACT.Sqrt).then_inc(sq_done, 1)
            act.wait_ge(wprep_pe, 1)
            nc.scalar.copy(wt[:].rearrange("p a d -> p (a d)"), bank[6][0:D, 0:3 * D])
            nc.scalar.copy(w3t[:], bank[7][0:D, :]).then_inc(wprep_act, 1)
            act.wait_ge(wprep_pe, 2)
            nc.scalar.copy(a12[:].rearrange("p a d -> p (a d)"), bank[6][0:D, 0:2 * D]).then_inc(wprep_act, 1)
            act.wait_ge(wprep_pe, 3)
            nc.scalar.copy(uvw[0:D, 0, :], bank[6][0:D, 128:128 + P])
            nc.scalar.copy(uvw[D:P, 1, :], bank[6][D:P, 128:128 + P])
            nc.scalar.copy(s_bias[:], bank[6][:, 0:1])
            nc.scalar.copy(g_sb[:].rearrange("p c d -> p (c d)"), bank[7][:, 0:FC * D]).then_inc(wprep_act, 1)

            def u_v_rows(h):
                n = HALVES[h][1]
                uv = bank[3 + h % 2][0:NP, 0:n * 4 * D].rearrange("p (i w d) -> p i w d", w=2, d=D)
                act.wait_ge(uv_ps_ready, h + 1)
                if h >= NR:
                    act.wait_ge(u_out_done[h % NR], 16 * (h // NR))
                    act.wait_ge(v_out_done[h % NR], 16 * (h // NR))
                nc.scalar.copy(v_parts[:, h % NR, 0:2 * n, 0, :], uv[:, :, 1, :]).then_inc(v_first, 1)
                nc.scalar.copy(u_out[:, h % NR, 0:2 * n, :], uv[:, :, 0, :]).then_inc(uv_ready, 1)

            def v_second(h):
                n = HALVES[h][1]
                act.wait_ge(v_rested, h + 1)
                nc.scalar.copy(v_parts[:, h % NR, 0:2 * n, 2, :], v_rest[:, h % 2, 0:2 * n, :]).then_inc(v_first, 1)

            for c in range(len(CHUNKS) + 2):
                if c < len(CHUNKS):
                    n = CHUNKS[c][1] * NP
                    act.wait_ge(ht_ps_ready, c + 1)
                    if c >= 2:
                        act.wait_ge(a_ps_ready, c - 1)
                    nc.scalar.activation(h_t[:, c % 2, 0:n], bank[c % 2][:, 0:n], ACT.Relu).then_inc(ht_ready, 1)
                if 1 <= c <= len(CHUNKS):
                    k = c - 1
                    n = CHUNKS[k][1] * NP
                    act.wait_ge(a_ps_ready, k + 1)
                    act.wait_ge(more_weights_in, 16 * N_MORE_WEIGHTS)
                    if k >= 2:
                        act.wait_ge(uv_ps_ready, HPC * (k - 1))
                    nc.scalar.activation(a_t[:, k % 2, 0:n], bank[(2, 5)[k % 2]][:, 0:n], ACT.Tanh,
                                         bias=b1col[:, 0:1]).then_inc(a_ready, 1)
                if c >= 2:
                    for h in range(HPC * (c - 2), min(HPC * (c - 1), len(HALVES))):
                        u_v_rows(h)
                        if h >= 1:
                            v_second(h - 1)
                    for k in range(2 * (c - 2), min(2 * (c - 1), 2 * TILES)):
                        act.wait_ge(cols_ps, k + 1)
                        dest = (src_gj if k < TILES else dst_gj)[:, :, k % TILES]
                        nc.scalar.copy(dest, bank[6 + k % 2][:, 0:NG]).then_inc(cols_read, 1)
            v_second(len(HALVES) - 1)

            act.wait_ge(flag_ready, 1)
            is_fast = act.value_load(fast[0:1, 0:1], min_val=0, max_val=1)

            def tanh_z(r):
                return nc.scalar.activation(tt_sb[:, r, :], z_ps, ACT.Tanh, bias=z_bias[:, 0:1])

            def copy_t(r):
                return nc.scalar.copy(t_sb[:, r, :, 0:D].rearrange("p (h q) c -> p q h c", h=2),
                                      t_ps.rearrange("p (q h c) -> p q h c", q=2, h=2))

            def copy_st(dest):
                tiles = dest.rearrange("p (q j e) -> p j q e", q=2, j=2)
                for j in range(2):
                    part = slice(j * D, (j + 1) * D)
                    for h in range(2):
                        last = nc.scalar.activation(tiles[h * D:(h + 1) * D, j], ut_ps[part].rearrange(
                            "p (q e) -> p q e", q=2), ACT.Identity, bias=s_bias[part, 0:1])
                return last

            def body(it, first, last):
                for u in range(UN):
                    if has(u, 0, first, last):
                        act.wait_ge(bt_ps_ready[u], count(it, u, 0))
                        if has(u, 2, first, False):
                            act.wait_ge(spread_ready[slot(u, 2)], count(it, u, 2))
                        nc.scalar.copy(bt_sb[:, u % 2, :], bt_ps).then_inc(bt_ready[u], 1)
                        nc.scalar.copy(idx_u[:, u, :], src_e[:, bass.ds(((it + 1) * UN + u) * TILES, TILES)]
                                       ).then_inc(idx_ready[u], 1)
                        if has(u, 2, first, False):
                            act.wait_ge(s2_ready[slot(u, 2)], count(it, u, 2))
                        copy_st(ut_sb[:, u % 2, :]).then_inc(ut_ready[u], 1)
                    if has(u, 2, first, last):
                        k = slot(u, 2)
                        act.wait_ge(z_ready[k], count(it, u, 2))
                        if has(u, 4, first, False):
                            act.wait_ge(t_ps_ready[slot(u, 4)], count(it, u, 4))
                        tanh_z(k % 2).then_inc(tt_ready[k], 1)
                        act.wait_ge(t_ps_ready[k], count(it, u, 2))
                        if has(u, 4, first, False):
                            act.wait_ge(seg_ready[slot(u, 4)], count(it, u, 4))
                        copy_t(k % 2).then_inc(t_ready[k], 1)

            with act.If(is_fast):
                for k in range(UN):
                    for s in (tt_ready, ut_ready, t_ready, bt_ready):
                        act.sem_inc(s[k], 1)
                body(0, True, False)
                with act.Fori(1, ITERS) as it:
                    body(it, False, False)
                body(ITERS, False, True)
            with act.Else():
                with act.Fori(0, NG) as g:
                    act.wait_ge(g_ps, g + 1)
                    copy_st(s2_sb[:, 0, :])
                    nc.scalar.copy(bt_sb[:, 0, :], bt_ps)
                    act.drain().then_inc(g_st, 1)
                    act.wait_ge(g_z, g + 1)
                    tanh_z(0).then_inc(g_tt, 1)
                    act.wait_ge(g_tps, g + 1)
                    copy_t(0).then_inc(g_t, 1)

        @block.vector
        def _(dve):
            x3 = x_sb[:, :].rearrange("p (i d) -> p i d", d=D)
            for i in range(NPP):
                if i % (NPP // 2) == 0:
                    dve.wait_ge(x_in[i // (NPP // 2)], 16)
                last = nc.vector.bn_stats(bn[:, i, :], x3[:, i, :])
            last.then_inc(ln, 1)
            dve.wait_ge(ln, 1)
            nc.vector.tensor_tensor(stats[:, 0, :], bn[:, :, 1], bn[:, :, 4], ALU.add)
            nc.vector.tensor_tensor(stats[:, 1, :], bn[:, :, 1], bn[:, :, 4], ALU.subtract)
            nc.vector.tensor_tensor(stats[:, 2, :], bn[:, :, 2], bn[:, :, 5], ALU.add).then_inc(ln, 1)
            dve.wait_ge(ln, 2)
            nc.vector.scalar_tensor_tensor(out=stats[:, 5, :], in0=stats[:, 1, :], scalar=0.25,
                                           in1=stats[:, 1, :], op0=ALU.mult, op1=ALU.mult)
            nc.vector.tensor_scalar(stats[:, 2, :], stats[:, 2, :], 1.0 / D, EPS, ALU.mult, ALU.add)
            nc.vector.tensor_scalar(stats[:, 0, :], stats[:, 0, :], 0.5, None, ALU.mult).then_inc(ln, 1)
            dve.wait_ge(ln, 3)
            nc.vector.tensor_tensor(stats[:, 3, :], stats[:, 2, :], stats[:, 5, :], ALU.add).then_inc(ln, 2)
            dve.wait_ge(consts, 2)
            nc.vector.tensor_copy(ident_b[:], ident[:])
            nc.vector.tensor_copy(iota_p[:, 0:1], iota_i[:, 0:1])
            nc.vector.tensor_scalar(iota_i[:, 1:2], iota_i[:, 0:1], NB - 1, None, ALU.bitwise_and).then_inc(ln, 1)
            dve.wait_ge(ln, 6)
            for k in (1, 2):
                nc.vector.tensor_scalar(iota_p[:, k:k + 1], iota_p[:, 0:1], float(k * W), float(W), ALU.is_ge,
                                        ALU.mult)
            nc.vector.tensor_copy(iota_8[:], iota_i[:, 1:2]).then_inc(ln, 1)
            dve.wait_ge(sq_done, 1)
            nc.vector.reciprocal(stats[:, 5, :], stats[:, 4, :]).then_inc(ln, 1)
            dve.wait_ge(ln, 8)
            nc.vector.tensor_tensor(iota_p[:, 1:2], iota_p[:, 1:2], iota_p[:, 2:3], ALU.add).then_inc(ln, 1)
            for c, (q0, n) in enumerate(CHUNKS):
                for i in range(2 * q0, 2 * (q0 + n)):
                    last = nc.vector.tensor_scalar(xn[:, i, :], x3[:, i, :], stats[:, 0, i:i + 1],
                                                   stats[:, 5, i:i + 1], ALU.subtract, ALU.mult)
                last.then_inc(normed_v, 1)
            dve.wait_ge(ln, 9)
            dve.wait_ge(consts, 3)
            nc.vector.tensor_tensor(iota_p[:, 0:1], iota_p[:, 0:1], iota_p[:, 1:2], ALU.subtract).then_inc(ln, 1)
            nc.vector.tensor_scalar(spread[:], iota_f[:, 0:NB].unsqueeze(2).to_broadcast([P, NB, D]),
                                    iota_8[:, 0:1], None, ALU.is_equal).then_inc(spread_made, 1)

            def split_v(halves):
                for h in halves:
                    n = HALVES[h][1]
                    uv = bank[3 + h % 2][0:NP, 0:n * 4 * D].rearrange("p (i w d) -> p i w d", w=2, d=D)
                    r, parts = v_rest[:, h % 2, 0:2 * n, :], v_parts[:, h % NR, 0:2 * n]
                    dve.wait_ge(v_first, 2 * h + 1)
                    dve.wait_ge(uv_ready, h + 1)
                    if h >= 2:
                        dve.wait_ge(v_split, h - 1)
                    nc.vector.tensor_tensor(r, uv[:, :, 1, :], parts[:, :, 0, :], ALU.subtract).then_inc(v_rested, 1)

            def finish_v(halves):
                for h in halves:
                    n = HALVES[h][1]
                    r, parts = v_rest[:, h % 2, 0:2 * n, :], v_parts[:, h % NR, 0:2 * n]
                    dve.wait_ge(v_first, min(2 * h + 3, 2 * len(HALVES)))
                    nc.vector.tensor_tensor(parts[:, :, 1, :], r, parts[:, :, 2, :], ALU.subtract).then_inc(v_split, 1)

            def rows_step(step):
                if step == 0:
                    dve.wait_ge(rows_f, 1)
                    nc.vector.tensor_reduce(out=rowst[:, 0, :], in_=dst_rows[:], axis=AX.X,
                                            op=ALU.min).then_inc(prep, 1)
                elif step == 1:
                    dve.wait_ge(prep, 1)
                    nc.vector.tensor_scalar(rowst[:, 2, :], rowst[:, 0, :], float(N - W), None,
                                            ALU.min).then_inc(prep, 1)
                    nc.vector.scalar_tensor_tensor(out=dst_cut, in0=dst_rows[:], scalar=float(N), in1=dst_rows[:],
                                                   op0=ALU.is_lt, op1=ALU.mult).then_inc(prep, 1)
                elif step == 2:
                    dve.wait_ge(prep, 3)
                    nc.vector.tensor_reduce(out=rowst[:, 1, :], in_=dst_cut, axis=AX.X,
                                            op=ALU.max).then_inc(prep, 1)
                    dve.wait_ge(prep, 4)
                    nc.vector.tensor_tensor(rowst[:, 3, :], rowst[:, 1, :], rowst[:, 2, :],
                                            ALU.subtract).then_inc(prep, 1)

            def windows():
                dve.wait_ge(starts_ps, 1)
                nc.vector.tensor_reduce(out=span1[:, 0:1], in_=bank[6][0:1, 0:NG], axis=AX.X,
                                        op=ALU.max).then_inc(starts_read, 1)
                nc.vector.tensor_copy(base_f[:], bank[7][0:1, 0:NG]).then_inc(starts_read, 1)
                dve.wait_ge(starts_read, 1)
                nc.vector.tensor_scalar(fast[:], span1[:, 0:1], float(W), None, ALU.is_lt).then_inc(flag_ready, 1)
                nc.vector.tensor_copy(base_row[:], bank[7][0:1, 0:NG]).then_inc(starts_read, 1)

            rows_step(0)
            for h in range(len(HALVES)):
                split_v([h])
                if h >= 1:
                    finish_v([h - 1])
                if h % 2 == 1:
                    rows_step((h + 1) // 2)
                if h == HPC * (C_STARTS - 1) - 1:
                    windows()
                    dve.wait_ge(flag_ready, 1)
                    is_fast = dve.value_load(fast[0:1, 0:1], min_val=0, max_val=1)
            finish_v([len(HALVES) - 1])
            dve.wait_ge(cols_read, 2 * TILES)
            dve.wait_ge(starts_ps, 2)
            nc.vector.tensor_tensor(loc_e[:, :].rearrange("p (g j) -> p g j", j=TILES), dst_gj,
                                    bank[6][:, 0:NG].unsqueeze(2).to_broadcast([P, NG, TILES]),
                                    ALU.subtract).then_inc(starts_read, 1)
            dve.wait_ge(starts_read, 4)
            def products(r):
                return nc.vector.tensor_tensor(
                    o_sb[:, r, :, :].rearrange("p c (j e) -> p j c e", j=TILES),
                    s2_sb[:, r, :].rearrange("p (j e) -> p j e", j=TILES).unsqueeze(2).to_broadcast(
                        [P, TILES, FC, P]),
                    spread_ps[:, :, :].rearrange("p j (c e) -> p j c e", c=FC), ALU.mult)

            def split_views(s):
                return b_parts[:, s:s + 2, :, :], b_rest[:, s // 2, :].rearrange("p (s t b) -> p s t b", s=2, b=NB)

            def split_values(n):
                return basis[:, bass.ds(n * NBT, 2 * NBT)].rearrange("p (s t b) -> p s t b", s=2, b=NB)

            def split_first(n, s, used):
                parts, _ = split_views(s)
                if used is not None:
                    dve.wait_ge(bt_ps_ready[s + 1], used)
                nc.vector.tensor_copy(parts[:, :, :, 0:NB], split_values(n)).then_inc(part1[s], 1)

            def split_rest(n, s, made):
                parts, left = split_views(s)
                dve.wait_ge(part1[s], made)
                nc.vector.tensor_tensor(left, split_values(n), parts[:, :, :, 0:NB], ALU.subtract
                                        ).then_inc(rest[s], 1)

            def split_second(s, made):
                parts, left = split_views(s)
                dve.wait_ge(rest[s], made)
                nc.vector.tensor_copy(parts[:, :, :, NB:2 * NB], left).then_inc(part2[s], 1)

            def split_third(s, made):
                parts, left = split_views(s)
                dve.wait_ge(part2[s], made)
                nc.vector.tensor_tensor(parts[:, :, :, 2 * NB:3 * NB], left, parts[:, :, :, NB:2 * NB],
                                        ALU.subtract).then_inc(part3[s], 1)

            def body(it, first, last):
                for u in range(UN):
                    n = it * UN + u
                    if has(u, 4, first, last):
                        k = slot(u, 4)
                        start = dve.value_load(base_row[0:1, bass.ds(n - UN, 1)], min_val=0, max_val=N - W)
                        window = acc[:, bass.ds(start, W)]
                        if has(u, 5, first, False):
                            dve.wait_ge(acc_done[slot(u, 5)], count(it, u, 5))
                        dve.wait_ge(seg_ready[k], count(it, u, 4))
                        nc.vector.tensor_tensor(window, window, seg_ps, ALU.add).then_inc(acc_done[k], 1)
                    split = u % 2 == 1 and has(u, 0, first, last)
                    if split:
                        split_first(n + 1, (u + 1) % UN,
                                    None if first and u + 2 < UN else count(it, u + 2, UN))
                    if has(u, 1, first, last):
                        k = slot(u, 1)
                        dve.wait_ge(ut_ready[k], count(it, u, 1))
                        dve.wait_ge(vt_ready[k], count(it, u, 1))
                        if has(u, 3, first, False):
                            dve.wait_ge(o_ready[slot(u, 3)], count(it, u, 3))
                        nc.vector.tensor_tensor(s2_sb[:, k % 2, :], ut_sb[:, k % 2, :], vt_ps,
                                                ALU.add).then_inc(s2_ready[k], 1)
                    if split:
                        split_rest(n + 1, (u + 1) % UN, count(it, u + 1, 0))
                    if has(u, 0, first, last):
                        dve.wait_ge(loc_in[u], 16 * dma_count(it, u, 0))
                        if has(u, 2, first, False):
                            dve.wait_ge(vt_ready[slot(u, 2)], count(it, u, 2))
                        nc.vector.tensor_scalar(hot_t[:, u % 2, :], loc_bc[:, u, :], iota_p[0:3 * W, 0:1], None,
                                                ALU.is_equal).then_inc(hot_t_ready[u], 1)
                    if split:
                        split_second((u + 1) % UN, count(it, u + 1, 0))
                    if has(u, 2, first, last):
                        k = slot(u, 2)
                        if has(u, 6, first, False):
                            dve.wait_ge(seg_ready[k], count(it, u, 6))
                        nc.vector.tensor_tensor(
                            hot[:, k, :, :],
                            loc_e[:, bass.ds((n - 2) * TILES, TILES)].unsqueeze(2).to_broadcast([P, TILES, W]),
                            iota_f[:, 0:W].unsqueeze(1).to_broadcast([P, TILES, W]),
                            ALU.is_equal).then_inc(hot_ready[k], 1)
                    if split:
                        split_third((u + 1) % UN, count(it, u + 1, 0))
                    if has(u, 1, first, last):
                        k = slot(u, 1)
                        dve.wait_ge(s2_ready[k], count(it, u, 1))
                        if has(u, 3, first, False):
                            dve.wait_ge(z_ready[slot(u, 3)], count(it, u, 3))
                        dve.wait_ge(spread_ready[k], count(it, u, 1))
                        products(k % 2).then_inc(o_ready[k], 1)

            with dve.If(is_fast):
                for k in range(UN):
                    for s in (hot_t_ready, hot_ready, s2_ready, part1, rest, part2, part3, o_ready, acc_done):
                        dve.sem_inc(s[k], 1)
                for k in range(UN):
                    nc.vector.tensor_copy(idx_u[:, k, :], src_e[:, k * TILES:(k + 1) * TILES]
                                          ).then_inc(idx_ready[k], 1)
                dve.wait_ge(basis_in, 16 * EARLY)
                split_first(0, 0, None)
                split_rest(0, 0, 2)
                split_second(0, 2)
                split_third(0, 2)
                body(0, True, False)
                with dve.Fori(1, NEED) as it:
                    body(it, False, False)
                dve.wait_ge(late_basis_in, 16 * (LATE + 1))
                with dve.Fori(NEED, ITERS) as it:
                    body(it, False, False)
                body(ITERS, False, True)
                for k in range(UN):
                    dve.wait_ge(acc_done[k], ITERS + 1)
            with dve.Else():
                dve.wait_ge(basis_in, 16 * EARLY)
                dve.wait_ge(late_basis_in, 16 * (LATE + 1))
                dve.sem_inc(g_seg, 1)
                with dve.Fori(0, NG) as g:
                    nc.vector.tensor_copy(idx_u[:, 0, :], src_e[:, bass.ds(g * TILES, TILES)])
                    nc.vector.tensor_copy(idx_v[:], dst_e[:, bass.ds(g * TILES, TILES)])
                    nc.vector.tensor_copy(dcur[:], dst_e[:, bass.ds(g * TILES, TILES)])
                    values = basis[:, bass.ds(g * NBT, NBT)].rearrange("p (t b) -> p t b", b=NB)
                    parts = b_parts[:, 0, :, :]
                    left = b_rest[:, 0, 0:NBT].rearrange("p (t b) -> p t b", b=NB)
                    nc.vector.tensor_copy(parts[:, :, 0:NB], values)
                    dve.drain()
                    nc.vector.tensor_scalar(idx_v[:], idx_v[:], float(N - 1), None, ALU.min).then_inc(g_idx, 1)
                    nc.vector.tensor_tensor(left, values, parts[:, :, 0:NB], ALU.subtract)
                    dve.drain()
                    nc.vector.tensor_copy(parts[:, :, NB:2 * NB], left)
                    dve.drain()
                    nc.vector.tensor_tensor(parts[:, :, 2 * NB:3 * NB], left, parts[:, :, NB:2 * NB],
                                            ALU.subtract).then_inc(g_parts, 1)
                    dve.wait_ge(g_rows, (g + 1) * (2 * TILES * 16))
                    nc.vector.tensor_tensor(s_sb[:], u_rows[:, 0], v_rows[:, :, 0, :], ALU.add)
                    for w in (2, 1):
                        dve.drain()
                        last = nc.vector.tensor_tensor(s_sb[:], s_sb[:], v_rows[:, :, w, :], ALU.add)
                    last.then_inc(g_s, 1)
                    dve.wait_ge(g_st, g + 1)
                    dve.wait_ge(g_spread, g + 1)
                    products(0).then_inc(g_o, 1)
                    dve.sem_inc(held, 1)
                    with dve.Fori(0, NBLK) as blk:
                        dve.wait_ge(g_seg, g * NBLK + blk + 1)
                        for j in range(TILES):
                            last = nc.vector.tensor_scalar(hot_blk[:, j, :], iota_f[:], dcur[:, j:j + 1], None,
                                                           ALU.is_equal)
                        last.then_inc(g_hot, 1)
                        dve.drain()
                        nc.vector.tensor_scalar(dcur[:], dcur[:], -float(BW), None, ALU.add)
                        dve.wait_ge(g_seg, g * NBLK + blk + 2)
                        block_sums = acc[:, bass.ds(blk * BW, BW)]
                        nc.vector.tensor_tensor(block_sums, block_sums, vt_ps[0:D + 1, :], ALU.add)
                        dve.drain()
            dve.drain().then_inc(acc_ready, 1)

            for c in range(7):
                n = min(8, NPP - 8 * c) * D
                dve.wait_ge(y_ps, c + 1)
                nc.vector.tensor_tensor(x_sb[:, c * 512:c * 512 + n], x_sb[:, c * 512:c * 512 + n],
                                        bank[c][0:NP, 0:n], ALU.add).then_inc(y_ready, 1)

        @block.tensor
        def _(pe):
            TWICE = (slice(0, D), slice(D, P))

            pe.wait_ge(consts, 2)
            pe.wait_ge(weights_in, 16 * N_WEIGHTS)
            for k in range(3):
                nc.tensor.transpose(bank[6][0:D, k * D:(k + 1) * D], wraw[:, k, :], ident[0:D, 0:D])
            for b in range(NB):
                last = nc.tensor.transpose(bank[7][0:D, b * D:(b + 1) * D],
                                           w3[:].rearrange("k (c b) -> k b c", b=NB)[:, b, :], ident[0:D, 0:D])
            last.then_inc(wprep_pe, 1)
            pe.wait_ge(wprep_act, 1)
            for k in range(2):
                last = nc.tensor.matmul(bank[6][0:D, k * D:(k + 1) * D], wt[:, 1 + k, :], p2[:], start=True,
                                        stop=True)
            last.then_inc(wprep_pe, 1)
            for c in range(FC):
                nc.tensor.matmul(bank[7][:, c * D:(c + 1) * D], w3t[:, c * P:(c + 1) * P], iw1[:], start=True,
                                 stop=True)
            pe.wait_ge(wprep_act, 2)
            for half in TWICE:
                const = bank[6][half, 0:1]
                nc.tensor.matmul(const, a12[:, 0, :], b2col[:], start=True, stop=False)
                nc.tensor.matmul(const, a12[:, 1, :], b2col[:], start=False, stop=False)
                nc.tensor.matmul(const, p2[:], pb1col[:], start=False, stop=False)
                nc.tensor.matmul(const, b2row[:], ones1[:, 0:1], start=False, stop=True)
                last = nc.tensor.matmul(bank[6][half, 128:128 + P], wt[:, 0, :],
                                        a12[:].rearrange("p a d -> p (a d)"), start=True, stop=True)
            last.then_inc(wprep_pe, 1)

            def columns(k):
                rows = src_rows if k < TILES else dst_rows
                pe.wait_ge(rows_f, 2)
                if k >= 2:
                    pe.wait_ge(cols_read, k - 1)
                for b in range(RB):
                    last = nc.tensor.transpose(
                        bank[6 + k % 2][:, b * RQ:(b + 1) * RQ],
                        rows[:, b, :].rearrange("q (p j) -> q j p", j=TILES)[:, k % TILES, :], ident[0:RQ, 0:RQ])
                last.then_inc(cols_ps, 1)

            def starts():
                pe.wait_ge(prep, 5)
                pe.wait_ge(cols_read, 2 * TILES)
                for b in range(RB):
                    for r, k in ((3, 6), (2, 7)):
                        last = nc.tensor.transpose(bank[k][0:1, b * RQ:(b + 1) * RQ], rowst[:, r, b:b + 1],
                                                   ident[0:RQ, 0:RQ])
                last.then_inc(starts_ps, 1)

            for c in range(len(CHUNKS) + 2):
                if c < len(CHUNKS):
                    q0, n = CHUNKS[c]
                    pe.wait_ge(normed_v, c + 1)
                    if c >= 2:
                        pe.wait_ge(ht_ready, c - 1)
                    for q in range(n):
                        last = nc.tensor.transpose(
                            bank[c % 2][:, q * NP:(q + 1) * NP],
                            xn[:, 2 * (q0 + q):2 * (q0 + q) + 2, :].rearrange("p i d -> p (i d)"),
                            ident[0:NP, 0:NP])
                    last.then_inc(ht_ps_ready, 1)
                if 1 <= c <= len(CHUNKS):
                    k = c - 1
                    n = CHUNKS[k][1] * NP
                    pe.wait_ge(ht_ready, k + 1)
                    if k >= 2:
                        pe.wait_ge(a_ready, k - 1)
                    if k == 0:
                        pe.wait_ge(more_weights_in, 16 * N_MORE_WEIGHTS)
                    nc.tensor.matmul(bank[(2, 5)[k % 2]][:, 0:n], w1[:], h_t[:, k % 2, 0:n], start=True,
                                     stop=True).then_inc(a_ps_ready, 1)
                if c >= 2:
                    k = c - 2
                    pe.wait_ge(a_ready, k + 1)
                    pe.wait_ge(wprep_act, 3)
                    for h in range(HPC * k, min(HPC * (k + 1), len(HALVES))):
                        q0, n = HALVES[h]
                        if h >= 2:
                            pe.wait_ge(uv_ready, h - 1)
                            pe.wait_ge(v_rested, h - 1)
                        for q in range(n):
                            at = (q0 + q - CHUNKS[k][0]) * NP
                            last = nc.tensor.matmul(bank[3 + h % 2][0:NP, q * 4 * D:(q + 1) * 4 * D],
                                                    a_t[:, k % 2, at:at + NP],
                                                    uvw[:].rearrange("p a c -> p (a c)"), start=True, stop=True)
                        last.then_inc(uv_ps_ready, 1)
                    for k in range(2 * (c - 2), min(2 * (c - 1), 2 * TILES)):
                        columns(k)
                    if c == C_STARTS:
                        starts()
                    if c == C_STARTS + 1:
                        pe.wait_ge(starts_read, 2)
                        nc.tensor.matmul(bank[6][:, 0:NG], ones1[:], base_f[:], start=True,
                                         stop=True).then_inc(starts_ps, 1)
            pe.wait_ge(starts_read, 4)
            pe.wait_ge(spread_made, 1)
            pe.wait_ge(uv_ready, len(HALVES))
            pe.wait_ge(v_split, len(HALVES))
            pe.wait_ge(consts, 3)
            pe.wait_ge(flag_ready, 1)
            is_fast = pe.value_load(fast[0:1, 0:1], min_val=0, max_val=1)

            def transpose_rows(rows):
                for q in range(2):
                    last = nc.tensor.transpose(ut_ps[:, q * P:(q + 1) * P],
                                               rows[:, 2 * q:2 * q + 2, :].rearrange("p j k -> p (j k)"), ident[:])
                return last

            def transpose_parts(k):
                return nc.tensor.matmul(bt_ps, b_parts[:, k, :, :].rearrange("p t q -> p (t q)"), ident_b[:],
                                        start=True, stop=True)

            def spread_basis(r):
                for c in range(FC):
                    for j in range(TILES):
                        q = slice(QT * j, QT * j + 3 * NB)
                        last = nc.tensor.matmul(spread_ps[:, j, c * P:(c + 1) * P],
                                                spread[q, 2 * c:2 * c + 2, :].rearrange("p b k -> p (b k)"),
                                                bt_sb[q, r, :], start=True, stop=True)
                return last

            def z_group(r):
                for c in range(FC):
                    for h in range(2):
                        last = nc.tensor.matmul(z_ps[h * D:(h + 1) * D, 0:2 * P], g_sb[:, c, :],
                                                o_sb[:, r, c, 2 * h * P:(2 * h + 2) * P],
                                                start=(c == 0), stop=(c == FC - 1))
                return last

            def t_transposes(r):
                for q in range(2):
                    last = nc.tensor.transpose(t_ps[:, q * P:(q + 1) * P], tt_sb[:, r, q * P:(q + 1) * P], ident[:])
                return last

            def body(it, first, last_pass):
                for u in range(UN):
                    if has(u, 0, first, last_pass):
                        pe.wait_ge(u_in[u], 64 * dma_count(it, u, 0))
                        if has(u, 1, first, False):
                            pe.wait_ge(ut_ready[slot(u, 1)], count(it, u, 1))
                        transpose_rows(u_rows[:, u]).then_inc(ut_ps_ready[u], 1)
                        pe.wait_ge(part3[u - u % 2], count(it, u, 0))
                        transpose_parts(u).then_inc(bt_ps_ready[u], 1)
                    if has(u, 1, first, last_pass):
                        k = slot(u, 1)
                        pe.wait_ge(bt_ready[k], count(it, u, 1))
                        if has(u, 2, first, False):
                            pe.wait_ge(o_ready[slot(u, 2)], count(it, u, 2))
                        spread_basis(k % 2).then_inc(spread_ready[k], 1)
                    if has(u, 2, first, last_pass):
                        k = slot(u, 2)
                        pe.wait_ge(o_ready[k], count(it, u, 2))
                        if has(u, 3, first, False):
                            pe.wait_ge(t_ready[slot(u, 3)], count(it, u, 3))
                        z_group(k % 2).then_inc(z_ready[k], 1)
                    if has(u, 0, first, last_pass):
                        pe.wait_ge(v_in[u], 16 * dma_count(it, u, 0))
                        if has(u, 1, first, False):
                            pe.wait_ge(s2_ready[slot(u, 1)], count(it, u, 1))
                        pe.wait_ge(hot_t_ready[u], count(it, u, 0))
                        for half in TWICE:
                            last = nc.tensor.matmul(vt_ps[half, :], v_win[:, u, :], hot_t[:, u % 2, :],
                                                    start=True, stop=True)
                        last.then_inc(vt_ready[u], 1)
                    if has(u, 3, first, last_pass):
                        k = slot(u, 3)
                        pe.wait_ge(t_ready[k], count(it, u, 3))
                        pe.wait_ge(hot_ready[k], count(it, u, 3))
                        if has(u, 4, first, False):
                            pe.wait_ge(acc_done[slot(u, 4)], count(it, u, 4))
                        for j in range(TILES):
                            last = nc.tensor.matmul(seg_ps, t_sb[:, k % 2, j, :], hot[:, k, j, :],
                                                    start=(j == 0), stop=(j == TILES - 1))
                        last.then_inc(seg_ready[k], 1)
                    if has(u, 2, first, last_pass):
                        k = slot(u, 2)
                        pe.wait_ge(tt_ready[k], count(it, u, 2))
                        t_transposes(k % 2).then_inc(t_ps_ready[k], 1)

            with pe.If(is_fast):
                for k in range(UN):
                    for s in (vt_ready, ut_ps_ready, bt_ps_ready, spread_ready, z_ready, t_ps_ready, seg_ready):
                        pe.sem_inc(s[k], 1)
                body(0, True, False)
                with pe.Fori(1, ITERS) as it:
                    body(it, False, False)
                body(ITERS, False, True)
            with pe.Else():
                with pe.Fori(0, NG) as g:
                    pe.wait_ge(g_s, g + 1)
                    pe.wait_ge(g_parts, g + 1)
                    transpose_rows(s_sb)
                    transpose_parts(0).then_inc(g_ps, 1)
                    pe.wait_ge(g_st, g + 1)
                    spread_basis(0).then_inc(g_spread, 1)
                    pe.wait_ge(g_o, g + 1)
                    z_group(0).then_inc(g_z, 1)
                    pe.wait_ge(g_tt, g + 1)
                    t_transposes(0).then_inc(g_tps, 1)
                    pe.wait_ge(g_t, g + 1)
                    pe.sem_inc(held, 1)
                    with pe.Fori(0, NBLK) as blk:
                        pe.wait_ge(g_hot, g * NBLK + blk + 1)
                        for j in range(TILES):
                            last = nc.tensor.matmul(vt_ps[0:D + 1, :], t_sb[:, 0, j, :], hot_blk[:, j, :],
                                                    start=(j == 0), stop=(j == TILES - 1))
                        last.then_inc(g_seg, 1)

            pe.wait_ge(acc_ready, 1)
            nodes = acc[:, 0:N].rearrange("c (p i) -> c i p", i=NPP)
            for c in range(7):
                for i in range(8 * c, min(8 * c + 8, NPP)):
                    for part in (slice(0, D), slice(D, NP)):
                        last = nc.tensor.matmul(bank[c][part, (i - 8 * c) * D:(i - 8 * c + 1) * D],
                                                nodes[:, i, part], w_out[:], start=True, stop=True)
                last.then_inc(y_ps, 1)


NAMES = ["x", "src", "dst", "edge_attr_8"] + ["L0_gnn_" + n for n in (
    "pp_W1", "pp_b1", "pp_W2", "pp_b2", "pi_W1", "pi_b1", "pi_W2", "pi_b2", "pi_W3", "ii_W1", "ii_b1", "ii_W2",
    "ii_b2")]


def kernel(**inputs):
    import concourse.bacc as bacc
    from concourse.bass_utils import run_bass_kernel_spmd

    nc = bacc.Bacc("TRN2", target_bir_lowering=False, num_devices=1)
    arrays = {n: np.ascontiguousarray(inputs[n]) for n in NAMES}
    aps = [nc.dram_tensor(n, arrays[n].shape, mybir.dt.from_np(arrays[n].dtype), kind="ExternalInput").ap()
           for n in NAMES]
    n_nodes, d = arrays["x"].shape
    f32 = mybir.dt.float32
    out = nc.dram_tensor("out", (n_nodes, d), f32, kind="ExternalOutput").ap()
    u_tab = nc.dram_tensor("u_tab", (n_nodes, d), f32).ap()
    v_tab = nc.dram_tensor("v_tab", (n_nodes, 3, d), mybir.dt.bfloat16).ap()
    loc_tab = nc.dram_tensor("loc_tab", (392, 512), mybir.dt.bfloat16).ap()
    program(nc, *aps, out, u_tab, v_tab, loc_tab)
    r = run_bass_kernel_spmd(nc, [arrays], core_ids=[0])
    return r.results[0]["out"]
```
